# Optimizing a Trainium2 kernel written in Bass

```python
import numpy as np
import jax
import jax.numpy as jnp

def _softmax(x, axis=-1):
    return jax.nn.softmax(x, axis=axis)

def _gelu(x):
    return jax.nn.gelu(x, approximate=True)

def _silu(x):
    return jax.nn.silu(x)

def _sigmoid(x):
    return jax.nn.sigmoid(x)

def _layernorm(x, axis=-1, eps=1e-05):
    m = jnp.mean(x, axis=axis, keepdims=True)
    v = jnp.var(x, axis=axis, keepdims=True)
    return (x - m) / jnp.sqrt(v + eps)

def _scatter_add(tgt, idx, src, axis=0):
    return tgt.at[idx].add(src)

def _segment_sum(src, seg, n):
    return jax.ops.segment_sum(src, seg, n)
kernel_name = 'mk_flamingo_gated_d2_seqx_r4_7e8e88'

def setup_inputs(seed: int=0):
    np.random.seed(seed)
    _w = jnp.asarray

    def _rec_inputs():
        import jax
        import jax.numpy as jnp
        _rk = jax.random.key(seed)
        x = -0.0002928 + 1 * jax.random.normal(jax.random.fold_in(_rk, 1), (8, 256, 256), jnp.float32)
        _lenS = 256 - jax.random.randint(jax.random.fold_in(_rk, 7), (8,), 0, max(1, 256 // 4) + 1, jnp.int32)
        _lenS2 = 256 - jax.random.randint(jax.random.fold_in(_rk, 8), (8,), 0, max(1, 256 // 4) + 1, jnp.int32)
        _ctx_1024P = jax.random.normal(jax.random.fold_in(_rk, 11), (8, 16, 256), jnp.float32)
        _ctx_1024c = jax.random.dirichlet(jax.random.fold_in(_rk, 511), 0.3 * jnp.ones((16,), jnp.float32), (8, 256))
        _ctx_1024t = jnp.einsum('bsk,bkd->bsd', _ctx_1024c, _ctx_1024P)
        _ctx_1024t = _ctx_1024t * jax.lax.rsqrt(jnp.mean(jnp.square(_ctx_1024t)) + 1e-12) * 0.953939
        ctx_1024 = -1.39393e-06 + 0.999914 * (_ctx_1024t + 0.3 * jax.random.normal(jax.random.fold_in(_rk, 611), (8, 256, 256), jnp.float32))
        _validS = jnp.arange(256)[None, :] < _lenS[:, None]
        _validS2 = jnp.arange(256)[None, :] < _lenS2[:, None]
        _causal = jnp.tril(jnp.ones((256, 256), dtype=bool))
        mask_Bx16xSxS2_ff0 = jnp.where(jnp.ones((8, 16, 256, 256), dtype=bool), 0.0, -1000000000.0).astype(jnp.float32)
        mask_1x1xSxS2_ik0 = jnp.where(jnp.broadcast_to(_validS2[0:1, None, None, :], (1, 1, 256, 256)), 0, 1).astype(jnp.int32)
        _g = jax.random.normal(jax.random.fold_in(_rk, 9001), (2, 2), jnp.float32)
        _g = jnp.sign(_g) * jnp.maximum(jnp.abs(_g), 1.0) + (_g == 0) * 1.0
        g_xattn = _g[0]
        g_ffn = _g[1]
        return (x, ctx_1024, mask_Bx16xSxS2_ff0, mask_1x1xSxS2_ik0, g_xattn, g_ffn)
    x, ctx_1024, mask_Bx16xSxS2_ff0, mask_1x1xSxS2_ik0, g_xattn, g_ffn = _rec_inputs()

    def _L0_xattn_setup():
        import jax, jax.numpy as jnp
        import numpy as np
        B, S, D = (2, 512, 256)
        H = 16
        DH = D // H
        LAMBDA_INIT = 0.8
        EPS = 1e-05
        SCALE = 1.0 / np.sqrt(DH)
        key = jax.random.key(seed)
        ks = jax.random.split(key, 13)
        inp = {'query': jax.random.normal(ks[0], (B, S, D), jnp.float32), 'key': jax.random.normal(ks[1], (B, S, D), jnp.float32), 'value': jax.random.normal(ks[2], (B, S, D), jnp.float32), 'attn_mask': jnp.zeros((B, H, S, S), jnp.float32), 'W_q': jax.random.normal(ks[3], (D, 2 * DH * H), jnp.float32) * 0.02, 'W_k': jax.random.normal(ks[4], (D, 2 * DH * H), jnp.float32) * 0.02, 'W_v': jax.random.normal(ks[5], (D, DH * H), jnp.float32) * 0.02, 'W_o': jax.random.normal(ks[6], (DH * H, D), jnp.float32) * 0.02, 'lambda_q1': jax.random.normal(ks[7], (H, DH), jnp.float32) * 0.1, 'lambda_k1': jax.random.normal(ks[8], (H, DH), jnp.float32) * 0.1, 'lambda_q2': jax.random.normal(ks[9], (H, DH), jnp.float32) * 0.1, 'lambda_k2': jax.random.normal(ks[10], (H, DH), jnp.float32) * 0.1, 'rms_scale': jnp.ones((DH,), jnp.float32)}
        return inp
    _L0_xattn_all = _L0_xattn_setup()
    _L0_xattn_in = {k: v for k, v in _L0_xattn_all.items() if k in ('W_q', 'W_k', 'W_v', 'W_o', 'lambda_q1', 'lambda_k1', 'lambda_q2', 'lambda_k2', 'rms_scale')}
    del _L0_xattn_all

    def _L0_ffn_setup():
        import jax, jax.numpy as jnp
        import numpy as np
        N_EXPERTS = 8
        TOP_K = 2
        D_MODEL = 256
        HIDDEN = 1024
        ROUTED_H = 256
        BATCH, SEQ = (2, 1024)
        key = jax.random.key(seed)
        ks = jax.random.split(key, 8)
        std = 0.02
        return {'x': jax.random.normal(ks[0], (BATCH, SEQ, D_MODEL), dtype=jnp.float32), 'w12': std * jax.random.normal(ks[1], (N_EXPERTS, 2 * ROUTED_H, D_MODEL), dtype=jnp.float32), 'w3': std * jax.random.normal(ks[2], (N_EXPERTS, D_MODEL, ROUTED_H), dtype=jnp.float32), 'shared_w1': std * jax.random.normal(ks[3], (HIDDEN, D_MODEL), dtype=jnp.float32), 'shared_w2': std * jax.random.normal(ks[4], (HIDDEN, D_MODEL), dtype=jnp.float32), 'shared_w3': std * jax.random.normal(ks[5], (D_MODEL, HIDDEN), dtype=jnp.float32), 'router_w': std * jax.random.normal(ks[6], (N_EXPERTS, D_MODEL), dtype=jnp.float32), 'expert_bias': jnp.zeros((N_EXPERTS,), dtype=jnp.float32)}
    _L0_ffn_all = _L0_ffn_setup()
    _L0_ffn_in = {k: v for k, v in _L0_ffn_all.items() if k in ('w12', 'w3', 'shared_w1', 'shared_w2', 'shared_w3', 'router_w', 'expert_bias')}
    del _L0_ffn_all

    def _L1_xattn_setup():
        import jax, jax.numpy as jnp
        import numpy as np
        B, S, D, H = (2, 512, 256, 16)
        DK = D // H

        def _split_heads(x):
            b, s, _ = x.shape
            return x.reshape(b, s, H, DK).transpose(0, 2, 1, 3)
        key = jax.random.key(seed)
        ks = jax.random.split(key, 7)
        q = jax.random.normal(ks[0], (B, S, D), dtype=jnp.float32)
        k = jax.random.normal(ks[1], (B, S, D), dtype=jnp.float32)
        v = jax.random.normal(ks[2], (B, S, D), dtype=jnp.float32)
        mask = jnp.tril(jnp.ones((S, S), dtype=jnp.int32))[None, None, :, :]
        scale = 1.0 / np.sqrt(DK)
        W_q = jax.random.normal(ks[3], (D, D), dtype=jnp.float32) * 0.02
        W_k = jax.random.normal(ks[4], (D, D), dtype=jnp.float32) * 0.02
        W_v = jax.random.normal(ks[5], (D, D), dtype=jnp.float32) * 0.02
        W_o = jax.random.normal(ks[6], (D, D), dtype=jnp.float32) * 0.02
        return {'q': q, 'k': k, 'v': v, 'mask': mask, 'W_q': W_q, 'W_k': W_k, 'W_v': W_v, 'W_o': W_o}
    _L1_xattn_all = _L1_xattn_setup()
    _L1_xattn_in = {k: v for k, v in _L1_xattn_all.items() if k in ('W_q', 'W_k', 'W_v', 'W_o')}
    del _L1_xattn_all

    def _L1_ffn_setup():
        import jax, jax.numpy as jnp
        import numpy as np
        NUM_EXPERTS = 8
        D_MODEL = 256
        D_FF = 1024
        BATCH, SEQ = (2, 1024)
        key = jax.random.key(seed)
        k_x, k_w1, k_w2 = jax.random.split(key, 3)
        x = jax.random.normal(k_x, (BATCH, SEQ, D_MODEL), dtype=jnp.float32)
        w1 = jax.random.normal(k_w1, (NUM_EXPERTS, D_MODEL, D_FF), dtype=jnp.float32) * (1.0 / np.sqrt(D_MODEL))
        b1 = jnp.zeros((NUM_EXPERTS, D_FF), dtype=jnp.float32)
        w2 = jax.random.normal(k_w2, (NUM_EXPERTS, D_FF, D_MODEL), dtype=jnp.float32) * (1.0 / np.sqrt(D_FF))
        b2 = jnp.zeros((NUM_EXPERTS, D_MODEL), dtype=jnp.float32)
        return {'x': x, 'w1': w1, 'b1': b1, 'w2': w2, 'b2': b2}
    _L1_ffn_all = _L1_ffn_setup()
    _L1_ffn_in = {k: v for k, v in _L1_ffn_all.items() if k in ('w1', 'b1', 'w2', 'b2')}
    del _L1_ffn_all
    return {'x': x, 'ctx_1024': ctx_1024, 'mask_Bx16xSxS2_ff0': mask_Bx16xSxS2_ff0, 'mask_1x1xSxS2_ik0': mask_1x1xSxS2_ik0, 'g_xattn': g_xattn, 'g_ffn': g_ffn, 'L0_xattn_W_q': _L0_xattn_in['W_q'], 'L0_xattn_W_k': _L0_xattn_in['W_k'], 'L0_xattn_W_v': _L0_xattn_in['W_v'], 'L0_xattn_W_o': _L0_xattn_in['W_o'], 'L0_xattn_lambda_q1': _L0_xattn_in['lambda_q1'], 'L0_xattn_lambda_k1': _L0_xattn_in['lambda_k1'], 'L0_xattn_lambda_q2': _L0_xattn_in['lambda_q2'], 'L0_xattn_lambda_k2': _L0_xattn_in['lambda_k2'], 'L0_xattn_rms_scale': _L0_xattn_in['rms_scale'], 'L0_ffn_w12': _L0_ffn_in['w12'], 'L0_ffn_w3': _L0_ffn_in['w3'], 'L0_ffn_shared_w1': _L0_ffn_in['shared_w1'], 'L0_ffn_shared_w2': _L0_ffn_in['shared_w2'], 'L0_ffn_shared_w3': _L0_ffn_in['shared_w3'], 'L0_ffn_router_w': _L0_ffn_in['router_w'], 'L0_ffn_expert_bias': _L0_ffn_in['expert_bias'], 'L1_xattn_W_q': _L1_xattn_in['W_q'], 'L1_xattn_W_k': _L1_xattn_in['W_k'], 'L1_xattn_W_v': _L1_xattn_in['W_v'], 'L1_xattn_W_o': _L1_xattn_in['W_o'], 'L1_ffn_w1': _L1_ffn_in['w1'], 'L1_ffn_b1': _L1_ffn_in['b1'], 'L1_ffn_w2': _L1_ffn_in['w2'], 'L1_ffn_b2': _L1_ffn_in['b2']}

def reference(x, ctx_1024, mask_Bx16xSxS2_ff0, mask_1x1xSxS2_ik0, g_xattn, g_ffn, L0_xattn_W_q, L0_xattn_W_k, L0_xattn_W_v, L0_xattn_W_o, L0_xattn_lambda_q1, L0_xattn_lambda_k1, L0_xattn_lambda_q2, L0_xattn_lambda_k2, L0_xattn_rms_scale, L0_ffn_w12, L0_ffn_w3, L0_ffn_shared_w1, L0_ffn_shared_w2, L0_ffn_shared_w3, L0_ffn_router_w, L0_ffn_expert_bias, L1_xattn_W_q, L1_xattn_W_k, L1_xattn_W_v, L1_xattn_W_o, L1_ffn_w1, L1_ffn_b1, L1_ffn_w2, L1_ffn_b2):
    import jax
    import jax.numpy as jnp

    def _L0_xattn_ref(query, key, value, attn_mask, W_q, W_k, W_v, W_o, lambda_q1, lambda_k1, lambda_q2, lambda_k2, rms_scale):
        import jax, jax.numpy as jnp
        import numpy as np
        B, S, D = (2, 512, 256)
        H = 16
        DH = D // H
        LAMBDA_INIT = 0.8
        EPS = 1e-05
        SCALE = 1.0 / np.sqrt(DH)
        b, s, _ = value.shape
        q = (query @ W_q).reshape(b, s, H, 2 * DH).transpose(0, 2, 1, 3)
        k = (key @ W_k).reshape(b, s, H, 2 * DH).transpose(0, 2, 1, 3)
        v = (value @ W_v).reshape(b, s, H, DH).transpose(0, 2, 1, 3)
        q1, q2 = (q[..., :DH], q[..., DH:])
        k1, k2 = (k[..., :DH], k[..., DH:])
        lam = jnp.exp(jnp.sum(lambda_q1 * lambda_k1, -1)) - jnp.exp(jnp.sum(lambda_q2 * lambda_k2, -1)) + LAMBDA_INIT
        lam = lam[None, :, None, None]
        s1 = jnp.einsum('bhqd,bhkd->bhqk', q1, k1) * SCALE + attn_mask
        s2 = jnp.einsum('bhqd,bhkd->bhqk', q2, k2) * SCALE + attn_mask
        attn = jax.nn.softmax(s1, axis=-1) - lam * jax.nn.softmax(s2, axis=-1)
        out = jnp.einsum('bhqk,bhkd->bhqd', attn, v)
        rms = jnp.sqrt(jnp.mean(out * out, axis=-1, keepdims=True) + EPS)
        out = out / rms * rms_scale
        out = out * (1.0 - LAMBDA_INIT)
        out = out.transpose(0, 2, 1, 3).reshape(b, s, H * DH)
        return out @ W_o

    def _L0_ffn_ref(x, w12, w3, shared_w1, shared_w2, shared_w3, router_w, expert_bias):
        import jax, jax.numpy as jnp
        import numpy as np
        N_EXPERTS = 8
        TOP_K = 2
        D_MODEL = 256
        HIDDEN = 1024
        ROUTED_H = 256
        BATCH, SEQ = (2, 1024)
        b, s, d = x.shape
        xf = x.reshape(-1, d)
        shared = jax.nn.silu(xf @ shared_w1.T) * (xf @ shared_w2.T) @ shared_w3.T
        scores = jax.nn.sigmoid(xf @ router_w.T)
        _, top_idx = jax.lax.top_k(scores + expert_bias, TOP_K)
        mask = jax.nn.one_hot(top_idx, N_EXPERTS, dtype=xf.dtype).sum(axis=-2)
        gates = scores * mask
        h12 = jnp.einsum('td,ehd->teh', xf, w12)
        h1, h2 = jnp.split(h12, 2, axis=-1)
        h = jax.nn.silu(h1) * h2 * gates[:, :, None]
        routed = jnp.einsum('teh,edh->td', h, w3)
        return (shared + routed).reshape(b, s, d)

    def _L1_xattn_ref(q, k, v, mask, W_q, W_k, W_v, W_o):
        import jax, jax.numpy as jnp
        import numpy as np
        B, S, D, H = (2, 512, 256, 16)
        DK = D // H

        def _split_heads(x):
            b, s, _ = x.shape
            return x.reshape(b, s, H, DK).transpose(0, 2, 1, 3)
        qh = _split_heads(q @ W_q.T)
        kh = _split_heads(k @ W_k.T)
        vh = _split_heads(v @ W_v.T)
        scores = jnp.einsum('bhqd,bhkd->bhqk', qh, kh) / np.sqrt(DK)
        scores = jnp.where(mask == 0, jnp.float32(-1000000000.0), scores)
        attn = jax.nn.softmax(scores, axis=-1)
        out = jnp.einsum('bhqk,bhkd->bhqd', attn, vh)
        out = out.transpose(0, 2, 1, 3).reshape(q.shape[0], q.shape[1], D)
        return out @ W_o.T

    def _L1_ffn_ref(x, w1, b1, w2, b2):
        import jax, jax.numpy as jnp
        import numpy as np
        NUM_EXPERTS = 8
        D_MODEL = 256
        D_FF = 1024
        BATCH, SEQ = (2, 1024)
        B, S, D = x.shape
        E = w1.shape[0]
        T = B * S // E
        tokens = x.reshape(E, T, D)
        h = jnp.einsum('etd,edf->etf', tokens, w1) + b1[:, None, :]
        h = jax.nn.gelu(h)
        y = jnp.einsum('etf,efd->etd', h, w2) + b2[:, None, :]
        return y.reshape(B, S, D)
    x = x + jnp.tanh(g_xattn[0]) * _L0_xattn_ref(_layernorm(x, axis=-1), ctx_1024, ctx_1024, mask_Bx16xSxS2_ff0, L0_xattn_W_q, L0_xattn_W_k, L0_xattn_W_v, L0_xattn_W_o, L0_xattn_lambda_q1, L0_xattn_lambda_k1, L0_xattn_lambda_q2, L0_xattn_lambda_k2, L0_xattn_rms_scale)
    x = x + jnp.tanh(g_ffn[0]) * _L0_ffn_ref(_layernorm(x, axis=-1), L0_ffn_w12, L0_ffn_w3, L0_ffn_shared_w1, L0_ffn_shared_w2, L0_ffn_shared_w3, L0_ffn_router_w, L0_ffn_expert_bias)
    x = x + jnp.tanh(g_xattn[1]) * _L1_xattn_ref(_layernorm(x, axis=-1), ctx_1024, ctx_1024, mask_1x1xSxS2_ik0, L1_xattn_W_q, L1_xattn_W_k, L1_xattn_W_v, L1_xattn_W_o)
    x = x + jnp.tanh(g_ffn[1]) * _L1_ffn_ref(_layernorm(x, axis=-1), L1_ffn_w1, L1_ffn_b1, L1_ffn_w2, L1_ffn_b2)
    return x

_drawn_inputs = setup_inputs


def setup_inputs(seed=0):
    import zlib

    import numpy as np

    out = dict(_drawn_inputs(seed))
    spreads = {'g_ffn': (-1.0, 0.6),
     'L0_xattn_rms_scale': (1.0, 0.6),
     'L0_ffn_expert_bias': (0.0, 0.671),
     'L1_ffn_b1': (0.0, 0.335),
     'L1_ffn_b2': (0.0, 0.405)}
    factors = {'L0_xattn_W_q': 4.112,
     'L0_xattn_W_k': 4.112,
     'L0_xattn_lambda_q1': 8.0,
     'L0_xattn_lambda_k1': 8.0,
     'L0_xattn_lambda_q2': 8.0,
     'L0_xattn_lambda_k2': 8.0,
     'L0_ffn_w12': 5.09,
     'L0_ffn_w3': 4.65,
     'L0_ffn_router_w': 7.269,
     'L1_xattn_W_q': 27.57,
     'L1_xattn_W_k': 27.414,
     'L0_ffn_shared_w1': 5.111,
     'L0_ffn_shared_w2': 5.061,
     'L0_ffn_shared_w3': 5.051,
     'L1_xattn_W_v': 2.84,
     'L1_xattn_W_o': 2.794}
    for name, (base, spread) in spreads.items():
        noise = np.random.default_rng([zlib.crc32(name.encode()), seed]).standard_normal(out[name].shape)
        drawn = base * np.exp(spread * noise) if base else spread * noise
        out[name] = jnp.asarray(drawn.astype(out[name].dtype))
    for name, factor in factors.items():
        out[name] = (out[name] * factor).astype(out[name].dtype)
    return out
```

```python
from contextlib import ExitStack

import concourse.bass as bass
from concourse import mybir

ALU = mybir.AluOpType
ACT = mybir.ActivationFunctionType
AX = mybir.AxisListType
F32 = mybir.dt.float32
F32R = mybir.dt.float32r
I32 = mybir.dt.int32

P = 128
B, S, D = 8, 256, 256
H, DH = 16, 16
NT = B * S // P
DC = D // P
ST = S // P
E = 8
FF = 1024
UH = 256
NU = FF // UH + E
FLT_MAX = 3.4028234663852886e38
MASKED = -1e30
LAMBDA_INIT = 0.8
EPS = 1e-5
SCALE = DH ** -0.5

BODY = 16
MASKS = 8
HALF = 8
FIRST, MIDDLE, LAST, DRAIN = range(4)


class Layer:

    def __init__(self, differential):
        self.differential = differential
        self.halves_per_batch = 2 if differential else 1
        self.heads_per_step = 1 if differential else 2
        self.heads_per_half = HALF * self.heads_per_step
        self.columns = 32 * HALF * self.halves_per_batch
        self.halves = B * self.halves_per_batch
        self.steps = HALF * self.halves
        self.bodies = self.steps // BODY
        self.batches_per_body = B // self.bodies

    def tasks(self, i, kind):
        if self.differential:
            table = {0: ("Q", 1), 2: ("K", 1), 4: ("V", 1), 5: ("xT", 2), 7: ("Q", 2), 9: ("K", 2), 11: ("oT", -1),
                     13: ("V", 2), 14: ("out", -1)}
            found = table.get(i)
        else:
            w, j = divmod(i, HALF)
            table = {0: ("Q", w + 1), 2: ("K", w + 1), 3: ("V", w + 1), 4: ("oT", w - 1), 5: ("xT", w + 2),
                     7: ("out", w - 1)}
            found = table.get(j)
        return [found] if found and self.exists(found[1], kind) else []

    def groups(self, i, kind):
        if self.differential:
            table = {0: (-1, 2), 4: (-1, 3), 8: (0, 0), 12: (0, 1)}
            found = table.get(i)
        else:
            w, j = divmod(i, HALF)
            table = {1: (w - 1, 2), 3: (w - 1, 3), 5: (w, 0), 7: (w, 1)}
            found = table.get(j)
        return [found] if found and self.exists(found[0], kind) else []

    @staticmethod
    def exists(half, kind):
        return {FIRST: half >= 0, MIDDLE: True, LAST: half < 2, DRAIN: half < 0}[kind]

    def opening(self):
        return [("xT", 0), ("Q", 0), ("K", 0), ("V", 0)] + [("xT", 1)] * (not self.differential)

    def previous(self, body, kind, i):
        if i:
            return body, kind, i - 1
        return {FIRST: None, MIDDLE: (body - 1, MIDDLE, BODY - 1), LAST: (self.bodies - 2, MIDDLE, BODY - 1),
                DRAIN: (self.bodies - 1, LAST, BODY - 1)}[kind]

    def number(self, name, i, kind, body):
        assert kind != DRAIN or i < BODY
        length = [sum(len(self.tasks(j, k)) for j in range(BODY)) for k in (FIRST, MIDDLE, LAST)]
        before = sum(len(self.tasks(j, kind)) for j in range(i))
        before += [n for n, _ in self.tasks(i, kind)].index(name) + len(self.opening())
        if kind != FIRST:
            before += length[0]
        if kind == MIDDLE:
            return (body - 1) * length[1] + before
        if kind == LAST:
            return before + length[1] * (self.bodies - 2)
        if kind == DRAIN:
            return before + length[1] * (self.bodies - 2) + length[2]
        return before

    @staticmethod
    def live(i, kind, lag):
        if kind == FIRST:
            return i >= lag
        if kind == LAST:
            return i - lag < BODY
        if kind == DRAIN:
            return i < lag
        return True

    def run(self, eng):
        yield 0, FIRST
        with eng.Fori(1, self.bodies - 1) as body:
            yield body, MIDDLE
        yield self.bodies - 1, LAST


def attention(nc, A, layer, mem, ctxT, mask, wq, wk, wv, wo):
    diff = layer.differential
    with ExitStack() as ctx:
        tag = "d" if diff else "p"

        def sb(name, shape, dt=F32):
            return ctx.enter_context(nc.sbuf_tensor(f"{tag}_{name}", shape, dt))

        def ps(name):
            return ctx.enter_context(nc.psum_tensor(f"{tag}_{name}", [P, 512], F32))

        def sem(name):
            return ctx.enter_context(nc.semaphore(f"{tag}_{name}"))

        MC = layer.columns
        X, ident, gate = mem["x"], mem["ident"], mem["gates"]
        raw_q, raw_k = sb("raw_q", [P, DC, MC]), sb("raw_k", [P, DC, MC])
        raw_v, raw_o = sb("raw_v", [P, DC, D]), sb("raw_o", [P, DC, D])
        Wq, Wk = sb("Wq", [P, 2, DC, MC], F32R), sb("Wk", [P, 2, DC, MC], F32R)
        Wv, Wo = sb("Wv", [P, 2, DC, D], F32R), sb("Wo", [P, 2, DC, D], F32R)
        xn = sb("xn", [P, ST, D])
        stats = sb("stats", [P, ST, 6])
        mv = sb("mv", [P, ST, 2])
        rstd = sb("rstd", [P, ST])
        xT = sb("xT", [P, 2, DC, S], F32R)
        raw_c = sb("raw_c", [P, DC, S])
        cT = sb("cT", [P, 2, DC, S], F32R)
        q_src, k_src = sb("q_src", [P, 2, 2, S], F32R), sb("k_src", [P, 2, 2, S], F32R)
        q_st, k_st = sb("q_st", [96, 2, 2, HALF, S], F32R), sb("k_st", [96, 2, HALF, S], F32R)
        V = sb("V", [P, 2, ST, layer.heads_per_half, 32])
        bias = sb("bias", [P, MASKS, ST, S]) if diff else sb("bias", [P, ST, S])
        Z = sb("Z", [P, 4, ST, 2, S])
        negmax = sb("negmax", [P, 4, ST, 2])
        sums = sb("sums", [P, 2, HALF, ST, 2])
        PT = sb("PT", [P, 2, ST, S])
        oT = sb("oT", [P, S])
        rinv = sb("rinv", [P, 2, ST, 4])
        O = sb("O", [P, ST, H, DH])
        OT = sb("OT", [P, 2, DC, S], F32R)
        if diff:
            comb = sb("comb", [P, 2, ST, S])
            rec2, coef = sb("rec2", [P, 2, ST]), sb("coef", [P, 2, ST])
            sq = sb("sq", [P, ST * H, DH])
            ms, rms = sb("ms", [P, ST * H]), sb("rms", [P, ST * H])
            ON = sb("ON", [P, ST, H, DH])
        else:
            ON = O
            raw_m = sb("raw_m", [P, ST, S], I32)
        psS = [[ps(f"scores{a}{q}") for q in range(ST)] for a in range(2)]
        psT = [ps(f"turned{a}") for a in range(2)]
        psO, psM = ps("summed"), ps("spare")

        q_dram, k_dram = (nc.dram_tensor(f"{tag}_{n}_scratch", [2, P, 2, 2 * S], F32).ap() for n in "qk")
        scratch_written = [sem(f"scratch_written{a}") for a in range(2)]
        w_loaded, w_high, w_split = sem("w_loaded"), sem("w_high"), sem("w_split")
        zeroed, passed = sem("zeroed"), sem("passed")
        x_loaded = mem["x_loaded"]
        ctx_loaded, ctx_high, ctx_split = sem("ctx_loaded"), sem("ctx_high"), sem("ctx_split")
        stats_half, stats_ready, eps_added = sem("stats_half"), sem("stats_ready"), sem("eps_added")
        rstd_ready, xn_ready = sem("rstd_ready"), sem("xn_ready")
        bank_filled, bank_emptied = sem("bank_filled"), sem("bank_emptied")
        stack_loaded = [sem(f"stack_loaded{a}") for a in range(2)]
        mask_loaded = [sem(f"mask_loaded{a}") for a in range(MASKS // 2)]
        scores_ready, masked, exp_ready = sem("scores_ready"), sem("masked"), sem("exp_ready")
        rec2_ready, coef_ready, combined = sem("rec2_ready"), sem("coef_ready"), sem("combined")
        turned, head_summed = sem("turned"), sem("head_summed")
        probsT_ready = [sem(f"probsT_ready{a}") for a in range(2)]
        oT_ready, rinv_ready = sem("oT_ready"), sem("rinv_ready")
        squared, ms_ready, ms_scaled, rms_ready, on_ready = (
            sem("squared"), sem("ms_ready"), sem("ms_scaled"), sem("rms_ready"), sem("on_ready"))
        bias_ready, wo_scaled = sem("bias_ready"), sem("wo_scaled")
        high = {n: sem(f"{n}_high") for n in ("xT", "Q", "K", "oT")}
        group_filled, group_emptied = sem("group_filled"), sem("group_emptied")
        split = {"xT": (xT, 1.0), "Q": (q_src, SCALE), "K": (k_src, 1.0), "oT": (OT, 1.0)}

        STACKED = 16 * 12
        HPS, HPH, HPB = layer.heads_per_step, layer.heads_per_half, layer.halves_per_batch
        NV = HPH * DH
        TAIL = BODY if diff else HALF + 1
        LEAVE, WEIGH = (3, 4) if diff else (2, 3)
        PARTS = ((0, 0), (0, 1), (1, 0))
        ctx_v = ctxT.rearrange("(c p) (b t) -> b p c t", p=P, t=S)

        def wait(eng, s, value):
            if not isinstance(value, int) or value > 0:
                eng.wait_ge(s, value)

        def hold(eng):
            eng.sem_inc(passed, 1)

        def f32(ap):
            return ap.bitcast(F32)

        def iterations(eng):
            for body, kind in layer.run(eng):
                for i in range(BODY):
                    yield body, kind, i
            for i in range(TAIL):
                yield layer.bodies, DRAIN, i

        def batch_of(body, half):
            return body + half // 2 if diff else 2 * body + half

        def tenants(body, i, m):
            return BODY * HPS // 2 * body + (HPS * i + m) // 2

        def uses(name, body, rel):
            return batch_of(body, rel) if name in ("xT", "oT") else 2 * body + rel

        block = ctx.enter_context(nc.Block())

        @block.sync
        def _(sp):
            if diff:
                for dst, src in mem["small_loads"]:
                    sp.dma_start(dst, src).then_inc(mem["small_loaded"], 16)
                xv = A["x"].rearrange("(n p) d -> p n d", p=P)
                sp.dma_start(X[:, 0:2, :], xv[:, 0:2, :]).then_inc(x_loaded, 16)
            sp.dma_start(raw_c[:], ctx_v[0]).then_inc(ctx_loaded, 16)
            for dst, src in ((raw_q, wq), (raw_k, wk), (raw_v, wv), (raw_o, wo)):
                sp.dma_start(dst[:], src.rearrange("(c p) n -> p c n", p=P)).then_inc(w_loaded, 16)
            if diff:
                sp.wait_ge(x_loaded, 16)
                sp.dma_start(X[:, 2:NT, :], xv[:, 2:NT, :]).then_inc(x_loaded, 16)
            else:
                sp.dma_start(raw_m[:], mask.rearrange("(t q) k -> q t k", q=P)).then_inc(mask_loaded[0], 16)

            def stack(slot, before):
                wait(sp, stack_loaded[slot], STACKED * before)
                hold(sp)
                for src, scratch in ((q_src, q_dram), (k_src, k_dram)):
                    sp.dma_start(scratch[slot], f32(src[:]).rearrange("p a t s -> p a (t s)"))\
                        .then_inc(scratch_written[slot], 16)
                sp.wait_ge(scratch_written[slot], 32 * (before + 1))
                hold(sp)
                for r, (hq, hk) in enumerate(((0, 0), (0, 1), (1, 0))):
                    for m in range(2):
                        rows = slice(48 * m + 16 * r, 48 * m + 16 * r + 16)
                        for dst, scratch, high in ((q_st[rows, slot, m], q_dram, hq), (k_st[rows, slot], k_dram, hk)):
                            sp.dma_start(f32(dst).rearrange("p (j t) s -> p j (t s)", t=2),
                                         scratch[slot, :, high].rearrange("(j m d) n -> m d j n", m=2, d=DH)[m])\
                                .then_inc(stack_loaded[slot], 16)

            def load_mask(batch, t, i):
                wait(sp, masked, 2 * (t + 2 - MASKS))
                hold(sp)
                sp.dma_start(bias[:, i % MASKS:i % MASKS + 2].rearrange("q h t k -> q (h t) k"),
                             mask[batch, i % H:i % H + 2].rearrange("h (t q) k -> q (h t) k", q=P))\
                    .then_inc(mask_loaded[i // 2 % (MASKS // 2)], 16)

            if diff:
                for i in range(0, MASKS - 2, 2):
                    load_mask(0, i, i)
            sp.wait_ge(zeroed, 1)
            sp.wait_ge(bank_emptied, 3)
            stack(0, 0)
            if not diff:
                sp.wait_ge(ctx_split, 1)
                sp.dma_start(raw_c[:], ctx_v[1]).then_inc(ctx_loaded, 16)
            for body, kind, i in iterations(sp):
                t = body * BODY + i
                ahead = i + MASKS - 2
                if diff and i % 2 == 0 and layer.live(i, kind, -(MASKS - 2)) and kind != DRAIN:
                    load_mask(body + ahead // BODY, t + MASKS - 2, ahead)
                for name, half in layer.tasks(i + 3, kind) if i + 3 < BODY else ():
                    if name == "V" and half % HPB == HPB - 1 and layer.exists(half + 1, kind):
                        batch = batch_of(body, half + 1)
                        sp.wait_ge(ctx_split, batch)
                        hold(sp)
                        sp.dma_start(raw_c[:], ctx_v[batch]).then_inc(ctx_loaded, 16)
                for name, half in layer.tasks(i - 1, kind) if i else ():
                    if name == "K":
                        sp.wait_ge(scores_ready, 2 * (body * BODY + HALF * (half - 1)))
                        hold(sp)
                        sp.wait_ge(bank_emptied, layer.number("K", i - 1, kind, body) + 1)
                        hold(sp)
                        stack(half % 2, body + half // 2)

        @block.gpsimd
        def _(pool):
            if diff:
                mem["constants"](pool)
            nc.gpsimd.memset(f32(q_st[:]), 0.0)
            nc.gpsimd.memset(V[:], 0.0).then_inc(zeroed, 1)

            def split_ctx(batch):
                pool.wait_ge(ctx_loaded, 16 * (batch + 1))
                hold(pool)
                nc.gpsimd.tensor_copy(cT[:, 0], raw_c[:]).then_inc(ctx_high, 1)
                pool.wait_ge(ctx_high, batch + 1)
                nc.gpsimd.tensor_tensor(cT[:, 1], raw_c[:], f32(cT[:, 0]), ALU.subtract).then_inc(ctx_split, 1)

            def root(batch):
                pool.wait_ge(stats_ready, batch + 1)
                hold(pool)
                nc.gpsimd.tensor_scalar(rstd[:], mv[:, :, 1], EPS, None, ALU.add).then_inc(eps_added, 1)
                pool.wait_ge(eps_added, batch + 1)
                nc.gpsimd.tensor_tensor(rstd[:], rstd[:], mem["minus_half"][:, 0:ST], ALU.pow).then_inc(rstd_ready, 1)

            root(0)
            split_ctx(0)
            if not diff:
                root(1)
            for n, (name, half) in enumerate(layer.opening()):
                if name == "V" and not diff:
                    pool.wait_ge(bank_filled, 4)
                    split_ctx(1)
            for body, kind, i in iterations(pool):
                for name, half in layer.tasks(i + 3, kind) if i + 3 < BODY else ():
                    if name == "xT":
                        root(batch_of(body, half))
                before = layer.previous(body, kind, i)
                for name, half in layer.tasks(before[2], before[1]) if before else ():
                    past, was, j = before
                    if name == "V" and half % HPB == HPB - 1 and layer.exists(half + 1, was):
                        pool.wait_ge(bank_filled, layer.number("V", j, was, past) + 1)
                        split_ctx(batch_of(past, half + 1))
                if diff and i == 5 and kind != FIRST:
                    pool.wait_ge(group_emptied, 4 * body)
                    O2 = O[:].rearrange("p a b c -> p (a b) c")
                    nc.gpsimd.tensor_tensor(sq[:], O2, O2, ALU.mult).then_inc(squared, 1)
                if diff and i == 6 and kind != FIRST:
                    pool.wait_ge(ms_ready, body)
                    hold(pool)
                    nc.gpsimd.tensor_scalar(rms[:], ms[:], 1.0 / DH, EPS, ALU.mult, ALU.add).then_inc(ms_scaled, 1)
                    pool.wait_ge(ms_scaled, body)
                    nc.gpsimd.tensor_tensor(rms[:], rms[:], mem["minus_half"][:], ALU.pow).then_inc(rms_ready, 1)

        @block.tensor
        def _(pe):
            def parts(out, left, right, cols_l, cols_r):
                for n, (a, b) in enumerate(PARTS):
                    for c in range(DC):
                        last = nc.tensor.matmul(out, left[:, a, c, cols_l], right[:, b, c, cols_r],
                                                start=(n == 0 and c == 0), stop=(n == 2 and c == DC - 1))
                return last

            def group(batch, g):
                pe.wait_ge(oT_ready, 4 * batch + g + 1)
                for q in range(ST):
                    last = nc.tensor.transpose(psO[:, S + q * P:S + (q + 1) * P], oT[:, q * P:(q + 1) * P], ident[:])
                last.then_inc(group_filled, 1)

            def task(name, rel, batch, n):
                wait(pe, bank_emptied, n)
                if name == "xT":
                    pe.wait_ge(xn_ready, batch + 1)
                    for q in range(ST):
                        for c in range(DC):
                            last = nc.tensor.transpose(psM[:, c * S + q * P:c * S + (q + 1) * P],
                                                       xn[:, q, c * P:(c + 1) * P], ident[:])
                if name in ("Q", "K"):
                    if name == "K":
                        pe.wait_ge(ctx_split, batch + 1)
                    w, src = (Wq, xT) if name == "Q" else (Wk, cT)
                    for t in range(2):
                        tile = 2 * (rel % HPB) + t
                        last = parts(psM[:, t * S:(t + 1) * S], w, src, slice(tile * P, (tile + 1) * P), slice(0, S))
                if name == "V":
                    pe.wait_ge(ctx_split, batch + 1)
                    for q in range(ST):
                        last = parts(psM[:, q * NV:(q + 1) * NV], cT, Wv, slice(q * P, (q + 1) * P),
                                     slice(rel % HPB * NV, (rel % HPB + 1) * NV))
                if name == "oT":
                    if diff:
                        pe.wait_ge(on_ready, batch + 1)
                    else:
                        pe.wait_ge(group_emptied, 4 * batch + 4)
                    rows = ON[:].rearrange("p q h d -> p q (h d)")
                    for q in range(ST):
                        for c in range(DC):
                            last = nc.tensor.transpose(psM[:, c * S + q * P:c * S + (q + 1) * P],
                                                       rows[:, q, c * P:(c + 1) * P], ident[:])
                if name == "out":
                    for q in range(ST):
                        last = parts(psM[:, q * D:(q + 1) * D], OT, Wo, slice(q * P, (q + 1) * P), slice(0, D))
                last.then_inc(bank_filled, 1)

            def scores(body, i):
                slot, s = i // HALF, i % HALF
                if s == 0:
                    pe.wait_ge(stack_loaded[slot], STACKED * (body + 1))
                for q in range(ST):
                    wait(pe, masked, 2 * (body * BODY + i - 2) + q + 1)
                    for m in range(2):
                        last = nc.tensor.matmul(psS[i % 2][q][:, m * S:(m + 1) * S],
                                                q_st[:, slot, m, s, q * P:(q + 1) * P], k_st[:, slot, s, :],
                                                start=True, stop=True)
                    last.then_inc(scores_ready, 1)

            def turn(body, i):
                t = body * BODY + i
                for m in range(HPS):
                    u = HPS * t + m
                    place = (HPS * i + m) % 2
                    wait(pe, probsT_ready[place], tenants(body, i, m))
                    if diff:
                        pe.wait_ge(combined, u + 1)
                        rows = comb[:, place]
                    else:
                        pe.wait_ge(exp_ready, 2 * t + 2)
                        rows = Z[:, i % 4, :, m, :]
                    for k in range(ST):
                        for q in range(ST):
                            last = nc.tensor.transpose(psT[place][:, k * S + q * P:k * S + (q + 1) * P],
                                                       rows[:, q, k * P:(k + 1) * P], ident[:])
                    last.then_inc(turned, 1)

            def weigh(body, i):
                for m in range(HPS):
                    u = HPS * (body * BODY + i) + m
                    place, j, v = (HPS * i + m) % 2, (HPS * i + m) % 4, (HPS * i + m) % HPH
                    pe.wait_ge(probsT_ready[place], tenants(body, i, m) + 1)
                    if j == 0:
                        wait(pe, group_emptied, BODY * HPS // 4 * body + HPS * i // 4)
                    for k in range(ST):
                        last = nc.tensor.matmul(psO[32 * j:32 * j + 32, 0:S], V[:, i // HALF % 2, k, v, :],
                                                PT[:, place, k, :], start=(k == 0), stop=(k == ST - 1),
                                                tile_position=(0, 32 * j))
                    last.then_inc(head_summed, 1)

            pe.wait_ge(mem["ident_ready"], 1)
            pe.wait_ge(w_split, 4)
            for n, (name, half) in enumerate(layer.opening()):
                task(name, half, batch_of(0, half), n)
            scores(0, 0)
            for body, kind, i in iterations(pe):
                t = body * BODY + i
                if kind != DRAIN and layer.live(i, kind, -1):
                    scores(body + (i + 1) // BODY, (i + 1) % BODY)
                for half, g in layer.groups(i, kind):
                    group(batch_of(body, half), g)
                for name, half in layer.tasks(i, kind) if diff else ():
                    task(name, half, batch_of(body, half), layer.number(name, i, kind, body))
                if layer.live(i, kind, 2):
                    turn(body - (i < 2), (i - 2) % BODY)
                if layer.live(i, kind, WEIGH):
                    weigh(body - (i < WEIGH), (i - WEIGH) % BODY)
                for name, half in layer.tasks(i, kind) if not diff else ():
                    task(name, half, batch_of(body, half), layer.number(name, i, kind, body))

        @block.scalar
        def _(act):
            if diff:
                mem["scalar_constants"](act)
            for n, (raw, w) in enumerate(((raw_q, Wq), (raw_k, Wk), (raw_v, Wv), (raw_o, Wo))):
                act.wait_ge(w_loaded, 64)
                if w is Wo and diff:
                    act.wait_ge(wo_scaled, 1)
                nc.scalar.activation(w[:, 0], raw[:], ACT.Copy).then_inc(w_high, 1)

            def task(name, rel, batch, n, body):
                if name == "out":
                    return
                act.wait_ge(bank_filled, n + 1)
                bank = psM[:].rearrange("p (a b) -> p a b", a=2)
                if name == "V":
                    act.wait_ge(zeroed, 1)
                    wait(act, head_summed, HPH * (2 * body + rel - 1))
                    for q in range(ST):
                        last = nc.scalar.activation(V[:, rel % 2, q, :, 0:DH],
                                                    psM[:, q * NV:(q + 1) * NV].rearrange("p (h d) -> p h d", d=DH),
                                                    ACT.Copy)
                    last.then_inc(bank_emptied, 1)
                    return
                if name in ("Q", "K"):
                    wait(act, scratch_written[(rel - 1) % 2], 32 * (body + (rel - 1) // 2 + 1))
                dst, scale = split[name]
                nc.scalar.activation(dst[:, 0], bank, ACT.Copy, scale=scale).then_inc(high[name], 1)

            for n, (name, half) in enumerate(layer.opening()):
                task(name, half, batch_of(0, half), n, 0)
            for body, kind, i in iterations(act):
                t = body * BODY + i

                def exps(q):
                    act.wait_ge(masked, 2 * t + q + 1)
                    for m in range(2):
                        last = nc.scalar.activation(Z[:, i % 4, q, m, :], Z[:, i % 4, q, m, :], ACT.Exp,
                                                    bias=negmax[:, i % 4, q, m:m + 1], scale=-1.0,
                                                    accum_out=sums[:, i // HALF, i % HALF, q, m:m + 1])
                    last.then_inc(exp_ready, 1)

                for half, g in layer.groups(i, kind):
                    act.wait_ge(head_summed, 4 * (4 * batch_of(body, half) + g + 1))
                    nc.scalar.activation(oT[:], psO[:, 0:S], ACT.Copy).then_inc(oT_ready, 1)
                if kind != DRAIN:
                    exps(0)
                before = layer.previous(body, kind, i)
                for name, half in layer.tasks(before[2], before[1]) if before else ():
                    past, was, j = before
                    task(name, half, batch_of(past, half), layer.number(name, j, was, past), past)
                if kind != DRAIN:
                    exps(1)
                if layer.live(i, kind, LEAVE):
                    u = HPS * (t - LEAVE)
                    place = HPS * (i - LEAVE) % 2
                    act.wait_ge(turned, u + 1)
                    wait(act, head_summed, u - 1)
                    nc.scalar.activation(PT[:, place].rearrange("p a b -> p (a b)"), psT[place][:], ACT.Copy)\
                        .then_inc(probsT_ready[place], 1)

        @block.vector
        def _(dve):
            if diff:
                mem["vector_constants"](dve)
                dve.wait_ge(w_loaded, 64)
                nc.vector.tensor_scalar(raw_o[:], raw_o[:], mem["rms_col"][:, 0:1], 1.0 - LAMBDA_INIT,
                                        ALU.mult, ALU.mult).then_inc(wo_scaled, 1)
            else:
                dve.wait_ge(mask_loaded[0], 16)
                nc.vector.tensor_scalar(bias[:], raw_m[:], 0.0, MASKED, ALU.is_equal, ALU.mult).then_inc(bias_ready, 1)

            def moments(batch):
                if diff:
                    dve.wait_ge(x_loaded, 16 if isinstance(batch, int) and batch == 0 else 32)
                for q in range(ST):
                    last = nc.vector.bn_stats(stats[:, q, :], X[:, bass.ds(2 * batch + q, 1), :])
                last.then_inc(stats_half, 1)
                dve.wait_ge(stats_half, batch + 1)
                hold(dve)
                for q in range(ST):
                    last = nc.vector.bn_aggr(mv[:, q, :], stats[:, q, :])
                last.then_inc(stats_ready, 1)

            def normalise(batch):
                dve.wait_ge(rstd_ready, batch + 1)
                for q in range(ST):
                    last = nc.vector.tensor_scalar(xn[:, q, :], X[:, bass.ds(2 * batch + q, 1), :], mv[:, q, 0:1],
                                                   rstd[:, q:q + 1], ALU.subtract, ALU.mult)
                last.then_inc(xn_ready, 1)

            def group(rel, batch, g):
                if True:
                    slot, s = rel % 2, 4 // HPS * g % HALF
                    if diff:
                        r = sums[:, slot, s:s + 4, :, 0].rearrange("p s q -> p q s")
                        dve.wait_ge(exp_ready, 2 * (4 * (4 * batch + g) + 4))
                        nc.vector.reciprocal(rinv[:, g % 2], r).then_inc(rinv_ready, 1)
                    else:
                        r = sums[:, slot, s:s + 2, :, :].rearrange("p s q m -> p q s m")
                        dve.wait_ge(exp_ready, 2 * (2 * (4 * batch + g) + 2))
                        nc.vector.reciprocal(rinv[:, g % 2].rearrange("p q (s m) -> p q s m", m=2), r).then_inc(rinv_ready, 1)
                    dve.wait_ge(rinv_ready, 4 * batch + g + 1)
                    dve.wait_ge(group_filled, 4 * batch + g + 1)
                    nc.vector.tensor_tensor(O[:, :, 4 * g:4 * g + 4, :],
                                            psO[:, S:S + ST * P].rearrange("p (q h d) -> p q h d", q=ST, d=32)[:, :, :, 0:DH],
                                            rinv[:, g % 2].unsqueeze(3).to_broadcast([P, ST, 4, DH]), ALU.mult)\
                        .then_inc(group_emptied, 1)

            def task(name, rel, batch, n, body):
                if name in split:
                    dst, scale = split[name]
                    dve.wait_ge(high[name], uses(name, body, rel) + 1)
                    nc.vector.scalar_tensor_tensor(out=dst[:, 1], in0=psM[:].rearrange("p (a b) -> p a b", a=2),
                                                   scalar=scale, in1=f32(dst[:, 0]), op0=ALU.mult, op1=ALU.subtract)\
                        .then_inc(bank_emptied, 1)
                if name == "out":
                    dve.wait_ge(bank_filled, n + 1)
                    rows = X[:, bass.ds(2 * batch, 2), :]
                    nc.vector.scalar_tensor_tensor(out=rows, in0=psM[:].rearrange("p (a b) -> p a b", a=2),
                                                   scalar=gate[:, layer.gate:layer.gate + 1], in1=rows,
                                                   op0=ALU.mult, op1=ALU.add).then_inc(bank_emptied, 1)

            moments(0)
            normalise(0)
            for n, (raw, w) in enumerate(((raw_q, Wq), (raw_k, Wk), (raw_v, Wv), (raw_o, Wo))):
                dve.wait_ge(w_high, n + 1)
                nc.vector.tensor_tensor(w[:, 1], raw[:], f32(w[:, 0]), ALU.subtract).then_inc(w_split, 1)
            for n, (name, half) in enumerate(layer.opening()):
                if (name, half) == ("xT", 1):
                    moments(1)
                    normalise(1)
                task(name, half, batch_of(0, half), n, 0)
            if not diff:
                dve.wait_ge(bias_ready, 1)
            for body, kind, i in iterations(dve):
                t = body * BODY + i
                new = kind in (FIRST, MIDDLE)
                late = t - 2
                for q in range(ST):
                    for half, g in layer.groups(i, kind) if q == 1 and not diff else ():
                        group(half, batch_of(body, half), g)
                    if kind != DRAIN:
                        dve.wait_ge(scores_ready, 2 * t + q + 1)
                    for m in range(2):
                        if kind != DRAIN:
                            if q == 0 and m == 0:
                                if diff:
                                    dve.wait_ge(mask_loaded[i // 2 % (MASKS // 2)], 16 * (BODY // MASKS * body + i // MASKS + 1))
                                else:
                                    wait(dve, turned, HPS * (t - 3))
                            if m == 0 and kind == MIDDLE:
                                hold(dve)
                            last = nc.vector.tensor_tensor_reduce(
                                Z[:, i % 4, q, m, :], psS[i % 2][q][:, m * S:(m + 1) * S],
                                bias[:, i % MASKS, q, :] if diff else bias[:, q, :], -1.0, FLT_MAX, ALU.add, ALU.min,
                                negmax[:, i % 4, q, m:m + 1])
                            if m == 1:
                                last.then_inc(masked, 1)
                        if not diff or not layer.live(i, kind, 2):
                            continue
                        h = (i - 2) % BODY
                        r = sums[:, h // HALF, h % HALF]
                        if (q, m) == (0, 0):
                            dve.wait_ge(exp_ready, 2 * late + 2)
                            nc.vector.reciprocal(rec2[:, h % 2, :], r[:, :, 1]).then_inc(rec2_ready, 1)
                        if (q, m) == (0, 1):
                            dve.wait_ge(rec2_ready, late + 1)
                            nc.vector.scalar_tensor_tensor(out=coef[:, h % 2, :], in0=rec2[:, h % 2, :],
                                                           scalar=mem["minus_lambda"][:, h:h + 1], in1=r[:, :, 0],
                                                           op0=ALU.mult, op1=ALU.mult).then_inc(coef_ready, 1)
                        if q == 1:
                            if m == 0:
                                dve.wait_ge(coef_ready, late + 1)
                                wait(dve, turned, late - 1)
                            last = nc.vector.scalar_tensor_tensor(
                                out=comb[:, h % 2, m, :], in0=Z[:, h % 4, m, 1, :], scalar=coef[:, h % 2, m:m + 1],
                                in1=Z[:, h % 4, m, 0, :], op0=ALU.mult, op1=ALU.add)
                            if m == 1:
                                last.then_inc(combined, 1)
                for name, half in layer.tasks(i + 3, kind) if i + 3 < BODY else ():
                    if name == "xT":
                        moments(batch_of(body, half))
                for name, half in layer.tasks(i + 1, kind) if i + 1 < BODY else ():
                    if name == "xT":
                        normalise(batch_of(body, half))
                if diff and i == 6 and kind != FIRST:
                    dve.wait_ge(squared, body)
                    nc.vector.tensor_reduce(ms[:], sq[:], AX.X, ALU.add).then_inc(ms_ready, 1)
                if diff and i == 8 and kind != FIRST:
                    dve.wait_ge(rms_ready, body)
                    nc.vector.tensor_tensor(ON[:].rearrange("p a b c -> p (a b) c"),
                                            O[:].rearrange("p a b c -> p (a b) c"),
                                            rms[:].unsqueeze(2).to_broadcast([P, ST * H, DH]), ALU.mult)\
                        .then_inc(on_ready, 1)
                if not diff and layer.live(i, kind, LEAVE):
                    u = HPS * (t - LEAVE) + 1
                    dve.wait_ge(turned, u + 1)
                    wait(dve, head_summed, u - 1)
                    nc.vector.tensor_copy(PT[:, 1].rearrange("p a b -> p (a b)"), psT[1][:]).then_inc(probsT_ready[1], 1)
                for half, g in layer.groups(i, kind) if diff else ():
                    group(half, batch_of(body, half), g)
                before = layer.previous(body, kind, i)
                for name, half in layer.tasks(before[2], before[1]) if before else ():
                    past, was, j = before
                    task(name, half, batch_of(past, half), layer.number(name, j, was, past), past)


def routed_ffn(nc, A, mem):
    TG = 512
    NG = B * S // TG
    TILES = TG // P
    UC = UH // P
    BODIES = NU // 2
    V_BODY, Q_BODY = 2 * NG, 2 * NG * UC
    with ExitStack() as ctx:
        def sb(name, shape, dt=F32):
            return ctx.enter_context(nc.sbuf_tensor(f"r_{name}", shape, dt))

        def sem(name):
            return ctx.enter_context(nc.semaphore(f"r_{name}"))

        X, ident, gates = mem["x"], mem["ident"], mem["gates"]
        stats, mv = sb("stats", [P, NT, 6]), sb("mv", [P, NT, 2])
        rstd = sb("rstd", [P, NT])
        xn = sb("xn", [P, 2, ST, D])
        xT = sb("xT", [P, 2, DC, B * S], F32R)
        raw_r = sb("raw_r", [P, DC, E])
        Wr = sb("Wr", [P, 2, DC, E], F32R)
        affinity = sb("affinity", [E, B * S])
        scores = sb("scores", [P, NT, E])
        chosen = sb("chosen", [P, NT, E])
        expert_bias = sb("expert_bias", [P, E])
        above, equal = sb("above", [P, NT, E, E]), sb("equal", [P, NT, E, E])
        earlier = sb("earlier", [P, E, E])
        gate = sb("gate", [P, NT, NU])
        raw_up, raw_down = sb("raw_up", [P, 2, DC, 2 * UH]), sb("raw_down", [P, 2, UC, D])
        Wup, Wdown = sb("Wup", [P, 2, 2, DC, 2 * UH], F32R), sb("Wdown", [P, 2, 2, UC, D], F32R)
        silu = sb("silu", [P, 2, TG])
        mixed = sb("mixed", [P, 2, TG])
        hidden = sb("hidden", [P, 2, 2, UC, TG], F32R)
        psH = [[ctx.enter_context(nc.psum_tensor(f"r_up{f}{k}", [P, TG], F32)) for k in range(2)] for f in range(2)]
        psD = [[ctx.enter_context(nc.psum_tensor(f"r_down{a}{k}", [P, 2 * D], F32)) for k in range(2)] for a in range(2)]

        small = sem("small")
        stats_ready, mv_ready, eps_added, rstd_ready = (sem("stats_ready"), sem("mv_ready"), sem("eps_added"),
                                                        sem("rstd_ready"))
        xn_ready, x_turned, x_high, x_split = sem("xn_ready"), sem("x_turned"), sem("x_high"), sem("x_split")
        wr_high, wr_split, routed, affinity_ready = sem("wr_high"), sem("wr_split"), sem("routed"), sem("affinity_ready")
        affinity_turned, chain = sem("affinity_turned"), sem("chain")
        ones_ready, earlier_ready = sem("ones_ready"), sem("earlier_ready")
        w_loaded = [sem(f"w_loaded{a}") for a in range(2)]
        w_part, w_split = sem("w_part"), sem("w_split")
        h1_ready, h2_ready, silu_ready, mixed_ready = sem("h1_ready"), sem("h2_ready"), sem("silu_ready"), sem("mixed_ready")
        high_ready, low_ready, down_ready, x_added = sem("high_ready"), sem("low_ready"), sem("down_ready"), sem("x_added")
        passed = sem("passed")
        PARTS = ((0, 0), (0, 1), (1, 0))

        def f32(ap):
            return ap.bitcast(F32)

        def wait(eng, s, value):
            if not isinstance(value, int) or value > 0:
                eng.wait_ge(s, value)

        def run(eng):
            yield 0, FIRST
            with eng.Fori(1, BODIES - 1) as body:
                yield body, MIDDLE
            yield BODIES - 1, LAST

        def pairs_of_batches(eng):
            for k in range(2):
                yield k, k
            with eng.Fori(1, B // 2) as pair:
                for k in range(2):
                    yield 2 * pair + k, k

        up_v = A["up"].rearrange("u (c p) n -> u p c n", p=P)
        down_v = A["down"].rearrange("u (f p) n -> u p f n", p=P)
        block = ctx.enter_context(nc.Block())

        @block.sync
        def _(sp):
            sp.dma_start(raw_r[:], A["router"].rearrange("(c p) e -> p c e", p=P)).then_inc(small, 16)
            sp.dma_start(expert_bias[:], A["L0_ffn_expert_bias"].partition_broadcast(P)).then_inc(small, 16)

            def load(unit, k):
                sp.dma_start(raw_up[:, k], up_v[unit]).then_inc(w_loaded[k], 16)
                sp.dma_start(raw_down[:, k], down_v[unit]).then_inc(w_loaded[k], 16)

            load(0, 0)
            load(1, 1)
            for body, kind in run(sp):
                for k in range(2):
                    if kind != LAST:
                        sp.wait_ge(w_split, 2 * body + k + 1)
                        sp.sem_inc(passed, 1)
                        load(2 * body + k + 2, k)

        @block.gpsimd
        def _(pool):
            nc.gpsimd.memset(earlier[:], 1.0).then_inc(ones_ready, 1)
            pool.wait_ge(ones_ready, 1)
            nc.gpsimd.affine_select(out=earlier[:], in_=earlier[:], compare_op=ALU.is_gt, fill=0.0, base=0,
                                    pattern=[[1, E], [-1, E]], channel_multiplier=0).then_inc(earlier_ready, 1)

            def split_part(n, k, w_parts):
                if n < 4:
                    raw, w = raw_up[:, k, n // 2], Wup[:, k, :, n // 2]
                else:
                    raw, w = raw_down[:, k], Wdown[:, k]
                if n % 2 == 0:
                    nc.gpsimd.tensor_copy(w[:, 0], raw).then_inc(w_part, 1)
                else:
                    pool.wait_ge(w_part, w_parts)
                    last = nc.gpsimd.tensor_tensor(w[:, 1], raw, f32(w[:, 0]), ALU.subtract)
                    if n == 5:
                        last.then_inc(w_split, 1)

            pool.wait_ge(w_loaded[0], 32)
            for n in range(6):
                split_part(n, 0, n // 2 + 1)
            pool.wait_ge(mv_ready, 1)
            nc.gpsimd.tensor_scalar(rstd[:], mv[:, :, 1], EPS, None, ALU.add).then_inc(eps_added, 1)
            pool.wait_ge(eps_added, 1)
            nc.gpsimd.tensor_tensor(rstd[:], rstd[:], mem["minus_half"][:, 0:NT], ALU.pow).then_inc(rstd_ready, 1)
            for body, kind in run(pool):
                for k in range(2):
                    for n in range(NG):
                        for f in range(UC):
                            q = body * Q_BODY + (k * NG + n) * UC + f
                            pool.wait_ge(high_ready, q + 1)
                            nc.gpsimd.tensor_tensor(hidden[:, n % 2, 1, f], mixed[:, f], f32(hidden[:, n % 2, 0, f]),
                                                    ALU.subtract).then_inc(low_ready, 1)
                            part = 2 * n + f - 1
                            if 0 <= part < 6 and not (kind == LAST and k == 1):
                                if part == 0:
                                    pool.wait_ge(w_loaded[1 - k], 32 * (body + k + 1))
                                    wait(pool, down_ready, NG * (2 * body + k))
                                    pool.sem_inc(passed, 1)
                                split_part(part, 1 - k, 3 * (2 * body + k + 1) + part // 2 + 1)

        @block.tensor
        def _(pe):
            for b, k in pairs_of_batches(pe):
                pe.wait_ge(xn_ready, b + 1)
                wait(pe, x_split, b - 1)
                for q in range(ST):
                    for c in range(DC):
                        last = nc.tensor.transpose(psH[k][0][:, c * S + q * P:c * S + (q + 1) * P],
                                                   xn[:, k, q, c * P:(c + 1) * P], ident[:])
                last.then_inc(x_turned, 1)
            pe.wait_ge(x_split, B)
            pe.wait_ge(wr_split, 1)
            for g in range(NG):
                for n, (a, b) in enumerate(PARTS + ((1, 1),)):
                    for c in range(DC):
                        last = nc.tensor.matmul(psD[g // 2][g % 2][0:E, :], Wr[:, a, c, :], xT[:, b, c, g * TG:(g + 1) * TG],
                                                start=(n == 0 and c == 0), stop=(n == 3 and c == DC - 1))
                last.then_inc(routed, 1)
            for t in range(NT):
                pe.wait_ge(affinity_ready, t // TILES + 1)
                last = nc.tensor.transpose(psH[1][1][:, t * E:(t + 1) * E], affinity[:, t * P:(t + 1) * P],
                                           ident[0:E, 0:E])
            last.then_inc(affinity_turned, 1)

            def up(v, k, n, body):
                for f in range(UC):
                    q = UC * v + f
                    wait(pe, mixed_ready, q - 1)
                    for half, ready in ((0, h1_ready), (1, h2_ready)):
                        for m, (a, b) in enumerate(PARTS):
                            for c in range(DC):
                                cols = slice(half * UH + f * P, half * UH + (f + 1) * P)
                                last = nc.tensor.matmul(psH[f][half][:], Wup[:, k, a, c, cols],
                                                        xT[:, b, c, n * TG:(n + 1) * TG],
                                                        start=(m == 0 and c == 0), stop=(m == 2 and c == DC - 1))
                        last.then_inc(ready, 1)

            def down(v, k, n):
                pe.wait_ge(low_ready, UC * v + UC)
                wait(pe, x_added, v - 1)
                for t in range(TILES):
                    for m, (a, b) in enumerate(PARTS):
                        for f in range(UC):
                            last = nc.tensor.matmul(psD[n % 2][t // 2][:, t % 2 * D:(t % 2 + 1) * D],
                                                    hidden[:, n % 2, a, f, t * P:(t + 1) * P], Wdown[:, k, b, f],
                                                    start=(m == 0 and f == 0), stop=(m == 2 and f == UC - 1))
                last.then_inc(down_ready, 1)

            pe.wait_ge(chain, 1)
            for body, kind in run(pe):
                for k in range(2):
                    for n in range(NG):
                        v = body * V_BODY + k * NG + n
                        if n == 0:
                            pe.wait_ge(w_split, 2 * body + k + 1)
                        up(v, k, n, body)
                        if not (kind == FIRST and k == 0 and n == 0):
                            down(v - 1, k if n else 1 - k, (n - 1) % NG)
            down(NU * NG - 1, 1, NG - 1)

        @block.scalar
        def _(act):
            act.wait_ge(small, 32)
            nc.scalar.activation(Wr[:, 0], raw_r[:], ACT.Copy).then_inc(wr_high, 1)
            for b, k in pairs_of_batches(act):
                act.wait_ge(x_turned, b + 1)
                nc.scalar.activation(xT[:, 0, :, bass.ds(S * b, S)], psH[k][0][:].rearrange("p (c s) -> p c s", c=DC),
                                     ACT.Copy).then_inc(x_high, 1)
            for g in range(NG):
                act.wait_ge(routed, g + 1)
                nc.scalar.activation(affinity[:, g * TG:(g + 1) * TG], psD[g // 2][g % 2][0:E, :], ACT.Sigmoid)\
                    .then_inc(affinity_ready, 1)

            def upper_half(v, f, n):
                q = UC * v + f
                act.wait_ge(mixed_ready, q + 1)
                if f == 0:
                    wait(act, down_ready, v - 1)
                nc.scalar.activation(hidden[:, n % 2, 0, f], mixed[:, f], ACT.Copy).then_inc(high_ready, 1)

            for body, kind in run(act):
                for k in range(2):
                    for n in range(NG):
                        v = body * V_BODY + k * NG + n
                        for f in range(UC):
                            q = UC * v + f
                            act.wait_ge(h1_ready, q + 1)
                            wait(act, mixed_ready, q - 1)
                            nc.scalar.activation(silu[:, f], psH[f][0][:], ACT.Silu).then_inc(silu_ready, 1)
                            if not (kind == FIRST and k == n == f == 0):
                                if f:
                                    upper_half(v, 0, n)
                                else:
                                    upper_half(v - 1, 1, (n - 1) % NG)
            upper_half(NU * NG - 1, 1, NG - 1)

        @block.vector
        def _(dve):
            for t in range(NT):
                last = nc.vector.bn_stats(stats[:, t, :], X[:, t, :])
            last.then_inc(stats_ready, 1)
            dve.wait_ge(stats_ready, 1)
            for t in range(NT):
                last = nc.vector.bn_aggr(mv[:, t, :], stats[:, t, :])
            last.then_inc(mv_ready, 1)
            dve.wait_ge(wr_high, 1)
            nc.vector.tensor_tensor(Wr[:, 1], raw_r[:], f32(Wr[:, 0]), ALU.subtract).then_inc(wr_split, 1)
            dve.wait_ge(rstd_ready, 1)
            for b, k in pairs_of_batches(dve):
                wait(dve, x_turned, b - 1)
                for q in range(ST):
                    t = 2 * b + q
                    last = nc.vector.tensor_scalar(xn[:, k, q, :], X[:, bass.ds(t, 1), :], mv[:, bass.ds(t, 1), 0],
                                                   rstd[:, bass.ds(t, 1)], ALU.subtract, ALU.mult)
                last.then_inc(xn_ready, 1)
                dve.wait_ge(x_high, b + 1)
                nc.vector.tensor_tensor(xT[:, 1, :, bass.ds(S * b, S)], psH[k][0][:].rearrange("p (c s) -> p c s", c=DC),
                                        f32(xT[:, 0, :, bass.ds(S * b, S)]), ALU.subtract).then_inc(x_split, 1)
            step = [0]

            def then(ins):
                step[0] += 1
                ins.then_inc(chain, 1)
                dve.wait_ge(chain, step[0])

            dve.wait_ge(affinity_turned, 1)
            then(nc.vector.tensor_copy(scores[:].rearrange("p t e -> p (t e)"), psH[1][1][:, 0:NT * E]))
            dve.wait_ge(small, 32)
            then(nc.vector.tensor_tensor(chosen[:], scores[:], expert_bias[:].unsqueeze(1).to_broadcast([P, NT, E]),
                                         ALU.add))
            other = chosen[:].unsqueeze(2).to_broadcast([P, NT, E, E])
            own = chosen[:].unsqueeze(3).to_broadcast([P, NT, E, E])
            then(nc.vector.tensor_tensor(above[:], other, own, ALU.is_gt))
            then(nc.vector.tensor_tensor(equal[:], other, own, ALU.is_equal))
            dve.wait_ge(earlier_ready, 1)
            then(nc.vector.tensor_tensor(equal[:], equal[:], earlier[:].unsqueeze(1).to_broadcast([P, NT, E, E]),
                                         ALU.mult))
            then(nc.vector.tensor_tensor(above[:], above[:], equal[:], ALU.add))
            then(nc.vector.tensor_reduce(chosen[:], above[:], AX.X, ALU.add))
            then(nc.vector.tensor_scalar(chosen[:], chosen[:], 1.5, None, ALU.is_lt))
            then(nc.vector.scalar_tensor_tensor(out=gate[:, :, NU - E:NU], in0=chosen[:], scalar=gates[:, 2:3],
                                                in1=scores[:], op0=ALU.mult, op1=ALU.mult))
            then(nc.vector.memset(gate[:, :, 0:NU - E], 1.0))
            then(nc.vector.tensor_scalar(gate[:, :, 0:NU - E], gate[:, :, 0:NU - E], gates[:, 2:3], None, ALU.mult))

            def add(v, unit_k, n, body):
                dve.wait_ge(down_ready, v + 1)
                for t in range(TILES):
                    rows = X[:, n * TILES + t, :]
                    last = nc.vector.scalar_tensor_tensor(
                        out=rows, in0=psD[n % 2][t // 2][:, t % 2 * D:(t % 2 + 1) * D],
                        scalar=gate[:, n * TILES + t, bass.ds(2 * body + unit_k, 1)], in1=rows, op0=ALU.mult, op1=ALU.add)
                last.then_inc(x_added, 1)

            for body, kind in run(dve):
                for k in range(2):
                    for n in range(NG):
                        v = body * V_BODY + k * NG + n
                        for f in range(UC):
                            q = UC * v + f
                            dve.wait_ge(silu_ready, q + 1)
                            dve.wait_ge(h2_ready, q + 1)
                            wait(dve, low_ready, q - 1)
                            nc.vector.tensor_tensor(mixed[:, f], psH[f][1][:], silu[:, f], ALU.mult)\
                                .then_inc(mixed_ready, 1)
                        if not (kind == FIRST and k == 0 and n == 0):
                            add(v - 1, k if n else k - 1, (n - 1) % NG, body)
            add(NU * NG - 1, 1, NG - 1, BODIES - 1)


def expert_ffn(nc, A, mem):
    FC = FF // P
    with ExitStack() as ctx:
        def sb(name, shape, dt=F32):
            return ctx.enter_context(nc.sbuf_tensor(f"e_{name}", shape, dt))

        def sem(name):
            return ctx.enter_context(nc.semaphore(f"e_{name}"))

        X, ident, gates = mem["x"], mem["ident"], mem["gates"]
        stats, mv = sb("stats", [P, NT, 6]), sb("mv", [P, NT, 2])
        rstd = sb("rstd", [P, NT])
        xn = sb("xn", [P, 2, ST, D])
        xT = sb("xT", [P, 2, DC, S])
        W1, W2 = sb("W1", [P, 2, DC, FF]), sb("W2", [P, 2, FC, D])
        b1_rows, b1 = sb("b1_rows", [E * FC, P]), sb("b1", [P, E * FC])
        b2 = sb("b2", [1, E, D])
        ones = sb("ones", [1, P])
        hidden = sb("hidden", [P, 2, FC, S])
        psX = [ctx.enter_context(nc.psum_tensor(f"e_x{a}", [P, DC * S], F32)) for a in range(2)]
        psH = [ctx.enter_context(nc.psum_tensor(f"e_h{a}", [P, 512], F32)) for a in range(4)]
        psY = [ctx.enter_context(nc.psum_tensor(f"e_y{a}", [P, ST * D], F32)) for a in range(2)]
        w_loaded = [sem(f"w_loaded{a}") for a in range(2)]
        small, ones_ready, b1_turned, b1_ready = sem("small"), sem("ones_ready"), sem("b1_turned"), sem("b1_ready")
        stats_ready, mv_ready, eps_added, rstd_ready = (sem("stats_ready"), sem("mv_ready"), sem("eps_added"),
                                                        sem("rstd_ready"))
        xn_ready, x_turned, xT_ready = sem("xn_ready"), sem("x_turned"), sem("xT_ready")
        h_ready, gelu_ready, y_ready, x_added, saved = (sem("h_ready"), sem("gelu_ready"), sem("y_ready"),
                                                        sem("x_added"), sem("saved"))
        passed = sem("passed")

        def wait(eng, s, value):
            if not isinstance(value, int) or value > 0:
                eng.wait_ge(s, value)

        def pairs(eng):
            for k in range(2):
                yield k, k
            with eng.Fori(1, B // 2) as pair:
                for k in range(2):
                    yield 2 * pair + k, k

        w1_v = A["L1_ffn_w1"].rearrange("e (c p) n -> e p c n", p=P)
        w2_v = A["L1_ffn_w2"].rearrange("e (f p) n -> e p f n", p=P)
        out_v = A["out"].rearrange("(b q p) d -> b p q d", p=P, q=ST)
        block = ctx.enter_context(nc.Block())

        def save(sp, b):
            sp.wait_ge(x_added, b + 1)
            sp.sem_inc(passed, 1)
            sp.dma_start(out_v[b], X[:, bass.ds(2 * b, 2), :]).then_inc(saved, 16)

        @block.sync
        def _(sp):
            sp.dma_start(b1_rows[:], A["L1_ffn_b1"].rearrange("e (f p) -> (e f) p", p=P)).then_inc(small, 16)
            sp.dma_start(b2[:], A["L1_ffn_b2"].rearrange("(a e) d -> a e d", a=1)).then_inc(small, 16)
            for b, k in pairs(sp):
                wait(sp, y_ready, b - 1)
                sp.sem_inc(passed, 1)
                sp.dma_start(W1[:, k], w1_v[b]).then_inc(w_loaded[k], 16)
                sp.dma_start(W2[:, k], w2_v[b]).then_inc(w_loaded[k], 16)
                if isinstance(b, int) and b < 1:
                    continue
                save(sp, b - 1)
            save(sp, B - 1)
            sp.wait_ge(saved, 16 * B)

        @block.gpsimd
        def _(pool):
            nc.gpsimd.memset(ones[:], 1.0).then_inc(ones_ready, 1)
            pool.wait_ge(mv_ready, 1)
            nc.gpsimd.tensor_scalar(rstd[:], mv[:, :, 1], EPS, None, ALU.add).then_inc(eps_added, 1)
            pool.wait_ge(eps_added, 1)
            nc.gpsimd.tensor_tensor(rstd[:], rstd[:], mem["minus_half"][:, 0:NT], ALU.pow).then_inc(rstd_ready, 1)

        @block.tensor
        def _(pe):
            pe.wait_ge(small, 32)
            pe.wait_ge(ones_ready, 1)
            nc.tensor.transpose(psY[1][:, 0:E * FC], b1_rows[:], ident[0:E * FC, 0:E * FC]).then_inc(b1_turned, 1)

            def turn(b, k):
                pe.wait_ge(xn_ready, b + 1)
                for q in range(ST):
                    for c in range(DC):
                        last = nc.tensor.transpose(psX[k][:, c * S + q * P:c * S + (q + 1) * P],
                                                   xn[:, k, q, c * P:(c + 1) * P], ident[:])
                last.then_inc(x_turned, 1)

            for b, k in pairs(pe):
                turn(b, k)
                pe.wait_ge(xT_ready, b + 1)
                pe.wait_ge(w_loaded[k], 32 * (b // 2 + 1) if isinstance(b, int) else 16 * (b - k + 2))
                for f in range(FC):
                    wait(pe, gelu_ready, FC * b + f - 7 + f % 2)
                    for c in range(DC):
                        last = nc.tensor.matmul(psH[f // 2][:, f % 2 * S:(f % 2 + 1) * S],
                                                W1[:, k, c, f * P:(f + 1) * P], xT[:, k, c, :],
                                                start=(c == 0), stop=(c == DC - 1))
                    if f % 2:
                        last.then_inc(h_ready, 1)
                wait(pe, x_added, b - 1)
                if isinstance(b, int) and b == 1:
                    pe.wait_ge(b1_ready, 1)
                for q in range(ST):
                    out = psY[k][:, q * D:(q + 1) * D]
                    for f in range(FC):
                        pe.wait_ge(gelu_ready, FC * b + f + 1)
                        nc.tensor.matmul(out, hidden[:, k, f, q * P:(q + 1) * P], W2[:, k, f, :],
                                         start=(f == 0), stop=False)
                    last = nc.tensor.matmul(out, ones[:], b2[:, bass.ds(b, 1), :], start=False, stop=True)
                last.then_inc(y_ready, 1)

        @block.scalar
        def _(act):
            act.wait_ge(b1_turned, 1)
            nc.scalar.activation(b1[:], psY[1][:, 0:E * FC], ACT.Copy).then_inc(b1_ready, 1)
            for b, k in pairs(act):
                act.wait_ge(x_turned, b + 1)
                wait(act, y_ready, b - 1)
                nc.scalar.activation(xT[:, k].rearrange("p c s -> p (c s)"), psX[k][:], ACT.Copy).then_inc(xT_ready, 1)
                act.wait_ge(b1_ready, 1)
                for f in range(FC):
                    act.wait_ge(h_ready, FC // 2 * b + f // 2 + 1)
                    nc.scalar.activation(hidden[:, k, f, :], psH[f // 2][:, f % 2 * S:(f % 2 + 1) * S],
                                         ACT.Gelu_apprx_tanh, bias=b1[:, bass.ds(FC * b + f, 1)])\
                        .then_inc(gelu_ready, 1)

        @block.vector
        def _(dve):
            for t in range(NT):
                last = nc.vector.bn_stats(stats[:, t, :], X[:, t, :])
            last.then_inc(stats_ready, 1)
            dve.wait_ge(stats_ready, 1)
            for t in range(NT):
                last = nc.vector.bn_aggr(mv[:, t, :], stats[:, t, :])
            last.then_inc(mv_ready, 1)
            dve.wait_ge(rstd_ready, 1)

            def normalise(b, k):
                wait(dve, x_turned, b - 1)
                for q in range(ST):
                    t = 2 * b + q
                    last = nc.vector.tensor_scalar(xn[:, k, q, :], X[:, bass.ds(t, 1), :], mv[:, bass.ds(t, 1), 0],
                                                   rstd[:, bass.ds(t, 1)], ALU.subtract, ALU.mult)
                last.then_inc(xn_ready, 1)

            def add(b, k):
                dve.wait_ge(y_ready, b + 1)
                rows = X[:, bass.ds(2 * b, 2), :]
                nc.vector.scalar_tensor_tensor(out=rows, in0=psY[k][:].rearrange("p (q d) -> p q d", q=ST),
                                               scalar=gates[:, 3:4], in1=rows, op0=ALU.mult, op1=ALU.add)\
                    .then_inc(x_added, 1)

            for b, k in pairs(dve):
                normalise(b, k)
                if not (isinstance(b, int) and b == 0):
                    add(b - 1, 1 - k)
            add(B - 1, 1)


def prepare(nc, A, mem):
    small_loaded, ramp, ident_ready, const_ready, lam_ready, gate_ready = (
        mem["small_loaded"], mem["ramp"], mem["ident_ready"], mem["const_ready"], mem["lam_ready"], mem["gate_ready"])

    def constants(pool):
        nc.gpsimd.memset(mem["ident"][:], 0.0).then_inc(ramp, 1)
        nc.gpsimd.memset(mem["minus_half"][:], -0.5).then_inc(ramp, 1)
        pool.wait_ge(ramp, 2)
        nc.gpsimd.affine_select(out=mem["ident"][:], in_=mem["ident"][:], compare_op=ALU.not_equal, fill=1.0, base=0,
                                pattern=[[-1, P]], channel_multiplier=1).then_inc(ident_ready, 1)

    def vector_constants(dve):
        lam, dots = mem["lam"], mem["dots"]
        dve.wait_ge(small_loaded, 16 * len(mem["small_loads"]))
        for n in range(2):
            nc.vector.tensor_tensor(lam[:, 2 * n, :], lam[:, 2 * n, :], lam[:, 2 * n + 1, :], ALU.mult)\
                .then_inc(lam_ready, 1)
        dve.wait_ge(lam_ready, 2)
        for n in range(2):
            nc.vector.tensor_reduce(dots[:, n, :], lam[:, 2 * n, :].rearrange("p (h d) -> p h d", d=DH), AX.X, ALU.add)\
                .then_inc(lam_ready, 1)
        dve.wait_ge(const_ready, 1)
        nc.vector.tensor_tensor(mem["minus_lambda"][:], dots[:, 1, :], dots[:, 0, :], ALU.subtract).then_inc(lam_ready, 1)
        dve.wait_ge(lam_ready, 5)
        nc.vector.tensor_scalar(mem["minus_lambda"][:], mem["minus_lambda"][:], LAMBDA_INIT, None, ALU.subtract)\
            .then_inc(lam_ready, 1)
        dve.wait_ge(lam_ready, 6)
        dve.wait_ge(gate_ready, 1)

    def scalar_constants(act):
        act.wait_ge(lam_ready, 4)
        nc.scalar.activation(mem["dots"][:], mem["dots"][:], ACT.Exp).then_inc(const_ready, 1)
        nc.scalar.activation(mem["gates"][:], mem["gates"][:], ACT.Tanh).then_inc(gate_ready, 1)

    mem["constants"], mem["vector_constants"], mem["scalar_constants"] = constants, vector_constants, scalar_constants


def build(nc, A, stop=None):
    with ExitStack() as ctx:
        def sb(name, shape, dt=F32):
            return ctx.enter_context(nc.sbuf_tensor(name, shape, dt))

        mem = {"x": sb("x", [P, NT, D]), "ident": sb("ident", [P, P]), "minus_half": sb("minus_half", [P, 32]),
               "gates": sb("gates", [P, 4]), "lam": sb("lam", [P, 4, H * DH]), "dots": sb("dots", [P, 2, H]),
               "minus_lambda": sb("minus_lambda", [P, H]), "rms_col": sb("rms_col", [P, 1])}
        for name in ("small_loaded", "ramp", "ident_ready", "const_ready", "lam_ready", "gate_ready", "x_loaded",
                     "saved"):
            mem[name] = ctx.enter_context(nc.semaphore(name))
        row = lambda a: a.partition_broadcast(P)
        mem["small_loads"] = [(mem["lam"][:, n, :], row(A[f"L0_xattn_lambda_{w}"].rearrange("h d -> (h d)")))
                              for n, w in enumerate(("q1", "k1", "q2", "k2"))]
        mem["small_loads"] += [(mem["gates"][:, 0:2], row(A["g_xattn"])), (mem["gates"][:, 2:4], row(A["g_ffn"]))]
        mem["small_loads"] += [(mem["rms_col"][DH * n:DH * (n + 1), :], A["L0_xattn_rms_scale"].rearrange("(d a) -> d a", a=1))
                               for n in range(P // DH)]
        prepare(nc, A, mem)
        first, second = Layer(True), Layer(False)
        first.gate, second.gate = 0, 1
        attention(nc, A, first, mem, A["ctxT"], A["mask_full"], A["L0_wq"], A["L0_wk"], A["L0_wv"], A["L0_wo"])
        if stop != "d":
            routed_ffn(nc, A, mem)
        if stop not in ("d", "r"):
            attention(nc, A, second, mem, A["ctxT"], A["mask_keys"], A["L1_wq"], A["L1_wk"], A["L1_wv"], A["L1_wo"])
        if stop is None:
            expert_ffn(nc, A, mem)
            return
        with nc.Block() as block:
            @block.sync
            def _(sp):
                sp.dma_start(A["out"].rearrange("(n p) d -> p n d", p=P), mem["x"][:]).then_inc(mem["saved"], 16)
                sp.wait_ge(mem["saved"], 16)


def tiled(w):
    return w.reshape(D, -1, 4, 2, 32).transpose(0, 1, 3, 2, 4).reshape(D, -1)


def layout(x, ctx_1024, mask_Bx16xSxS2_ff0, mask_1x1xSxS2_ik0, g_xattn, g_ffn, **w):
    import numpy as np

    turn = lambda a: np.swapaxes(a, -1, -2)
    up = [np.concatenate([turn(w["L0_ffn_shared_w1"])[:, u * UH:(u + 1) * UH],
                          turn(w["L0_ffn_shared_w2"])[:, u * UH:(u + 1) * UH]], 1) for u in range(FF // UH)]
    down = [turn(w["L0_ffn_shared_w3"])[u * UH:(u + 1) * UH] for u in range(FF // UH)]
    arrays = {
        "x": x.reshape(B * S, D), "ctxT": turn(ctx_1024.reshape(B * S, D)), "mask_full": mask_Bx16xSxS2_ff0,
        "mask_keys": mask_1x1xSxS2_ik0[0, 0], "g_xattn": g_xattn, "g_ffn": g_ffn,
        "L0_wq": tiled(w["L0_xattn_W_q"]), "L0_wk": tiled(w["L0_xattn_W_k"]),
        "L0_wv": w["L0_xattn_W_v"], "L0_wo": w["L0_xattn_W_o"],
        "L1_wq": tiled(turn(w["L1_xattn_W_q"])), "L1_wk": tiled(turn(w["L1_xattn_W_k"])),
        "L1_wv": turn(w["L1_xattn_W_v"]), "L1_wo": turn(w["L1_xattn_W_o"]),
        "up": np.concatenate([np.stack(up), turn(w["L0_ffn_w12"])]),
        "down": np.concatenate([np.stack(down), turn(w["L0_ffn_w3"])]),
        "router": turn(w["L0_ffn_router_w"]),
    }
    for name in ("L0_xattn_lambda_q1", "L0_xattn_lambda_k1", "L0_xattn_lambda_q2", "L0_xattn_lambda_k2",
                 "L0_xattn_rms_scale", "L0_ffn_expert_bias", "L1_ffn_w1", "L1_ffn_b1", "L1_ffn_w2", "L1_ffn_b2"):
        arrays[name] = w[name]
    return {name: np.ascontiguousarray(a) for name, a in arrays.items()}


def kernel(**inputs):
    import numpy as np
    import concourse.bacc as bacc
    from concourse.bass_utils import run_bass_kernel_spmd

    nc = bacc.Bacc("TRN2", target_bir_lowering=False, num_devices=1)
    arrays = {f"in_{n}": a for n, a in layout(**{n: np.asarray(a) for n, a in inputs.items()}).items()}
    A = {n[3:]: nc.dram_tensor(n, a.shape, mybir.dt.from_np(a.dtype), kind="ExternalInput").ap()
         for n, a in arrays.items()}
    A["out"] = nc.dram_tensor("out", (B * S, D), F32, kind="ExternalOutput").ap()
    build(nc, A)
    r = run_bass_kernel_spmd(nc, [arrays], core_ids=[0])
    return r.results[0]["out"].reshape(B, S, D)
```

```python
from contextlib import ExitStack

import concourse.bass as bass
from concourse import mybir

ALU = mybir.AluOpType
ACT = mybir.ActivationFunctionType
AX = mybir.AxisListType
F32 = mybir.dt.float32
F32R = mybir.dt.float32r
I32 = mybir.dt.int32

P = 128
B, S, D = 8, 256, 256
H, DH = 16, 16
NT = B * S // P
DC = D // P
ST = S // P
E = 8
FF = 1024
UH = 256
NU = FF // UH + E
FLT_MAX = 3.4028234663852886e38
MASKED = -1e30
LAMBDA_INIT = 0.8
EPS = 1e-5
SCALE = DH ** -0.5

BODY = 16
MASKS = 8
HALF = 8
FIRST, MIDDLE, LAST, DRAIN = range(4)


class Layer:

    def __init__(self, differential):
        self.differential = differential
        self.halves_per_batch = 2 if differential else 1
        self.heads_per_step = 1 if differential else 2
        self.heads_per_half = HALF * self.heads_per_step
        self.columns = 32 * HALF * self.halves_per_batch
        self.halves = B * self.halves_per_batch
        self.steps = HALF * self.halves
        self.bodies = self.steps // BODY
        self.batches_per_body = B // self.bodies

    def tasks(self, i, kind):
        if self.differential:
            table = {0: ("Q", 1), 1: ("K", 1), 3: ("V", 1), 4: ("xT", 2), 6: ("Q", 2), 8: ("K", 2), 10: ("oT", -1),
                     12: ("V", 2), 14: ("out", -1)}
            found = table.get(i)
        else:
            w, j = divmod(i, HALF)
            table = {0: ("Q", w + 1), 1: ("K", w + 1), 3: ("V", w + 1), 4: ("oT", w - 1), 5: ("xT", w + 2),
                     6: ("out", w - 1)}
            found = table.get(j)
        return [found] if found and self.exists(found[1], kind) else []

    def groups(self, i, kind):
        if self.differential:
            table = {0: (-1, 2), 4: (-1, 3), 8: (0, 0), 12: (0, 1)}
            found = table.get(i)
        else:
            w, j = divmod(i, HALF)
            table = {1: (w - 1, 2), 3: (w - 1, 3), 5: (w, 0), 7: (w, 1)}
            found = table.get(j)
        return [found] if found and self.exists(found[0], kind) else []

    @staticmethod
    def exists(half, kind):
        return {FIRST: half >= 0, MIDDLE: True, LAST: half < 2, DRAIN: half < 0}[kind]

    def opening(self):
        return [("xT", 0), ("K", 0), ("Q", 0), ("V", 0)] + [("xT", 1)] * (not self.differential)

    def previous(self, body, kind, i):
        if i:
            return body, kind, i - 1
        return {FIRST: None, MIDDLE: (body - 1, MIDDLE, BODY - 1), LAST: (self.bodies - 2, MIDDLE, BODY - 1),
                DRAIN: (self.bodies - 1, LAST, BODY - 1)}[kind]

    def number(self, name, i, kind, body):
        assert kind != DRAIN or i < BODY
        length = [sum(len(self.tasks(j, k)) for j in range(BODY)) for k in (FIRST, MIDDLE, LAST)]
        before = sum(len(self.tasks(j, kind)) for j in range(i))
        before += [n for n, _ in self.tasks(i, kind)].index(name) + len(self.opening())
        if kind != FIRST:
            before += length[0]
        if kind == MIDDLE:
            return (body - 1) * length[1] + before
        if kind == LAST:
            return before + length[1] * (self.bodies - 2)
        if kind == DRAIN:
            return before + length[1] * (self.bodies - 2) + length[2]
        return before

    @staticmethod
    def live(i, kind, lag):
        if kind == FIRST:
            return i >= lag
        if kind == LAST:
            return i - lag < BODY
        if kind == DRAIN:
            return i < lag
        return True

    def run(self, eng):
        yield 0, FIRST
        with eng.Fori(1, self.bodies - 1) as body:
            yield body, MIDDLE
        yield self.bodies - 1, LAST


def attention(nc, A, layer, mem, ctxT, mask, wq, wk, wv, wo, next_loads=()):
    diff = layer.differential
    with ExitStack() as ctx:
        tag = "d" if diff else "p"

        def sb(name, shape, dt=F32):
            return ctx.enter_context(nc.sbuf_tensor(f"{tag}_{name}", shape, dt))

        def ps(name):
            return ctx.enter_context(nc.psum_tensor(f"{tag}_{name}", [P, 512], F32))

        def sem(name):
            return ctx.enter_context(nc.semaphore(f"{tag}_{name}"))

        MC = layer.columns
        X, ident, gate = mem["x"], mem["ident"], mem["gates"]
        raw_q, raw_k = sb("raw_q", [P, DC, MC]), sb("raw_k", [P, DC, MC])
        raw_v, raw_o = sb("raw_v", [P, DC, D]), sb("raw_o", [P, DC, D])
        Wq, Wk = sb("Wq", [P, 2, DC, MC], F32R), sb("Wk", [P, 2, DC, MC], F32R)
        Wv, Wo = sb("Wv", [P, 2, DC, D], F32R), sb("Wo", [P, 2, DC, D], F32R)
        xn = sb("xn", [P, ST, D])
        stats = sb("stats", [P, ST, 6])
        mv = sb("mv", [P, ST, 2])
        rstd = sb("rstd", [P, ST])
        xT = sb("xT", [P, 2, DC, S], F32R)
        raw_c = sb("raw_c", [P, DC, S])
        cT = sb("cT", [P, 2, DC, S], F32R)
        q_src, k_src = sb("q_src", [P, 2, 2, S], F32R), sb("k_src", [P, 2, 2, S], F32R)
        q_st, k_st = sb("q_st", [96, 2, 2, HALF, S], F32R), sb("k_st", [96, 2, HALF, S], F32R)
        V = sb("V", [P, 2, ST, layer.heads_per_half, 32])
        bias = sb("bias", [P, MASKS, ST, S]) if diff else sb("bias", [P, ST, S])
        Z = sb("Z", [P, 4, ST, 2, S])
        negmax = sb("negmax", [P, 4, ST, 2])
        sums = sb("sums", [P, 2, HALF, ST, 2]) if diff else None
        PT = sb("PT", [P, 4, ST, S])
        oT = sb("oT", [P, S])
        rinv = sb("rinv", [P, 2, ST, 4])
        O = sb("O", [P, ST, H, DH])
        OT = sb("OT", [P, 2, DC, S], F32R)
        if diff:
            comb = sb("comb", [P, 2, ST, S])
            rec2, coef = sb("rec2", [P, 2, ST]), sb("coef", [P, 2, ST])
            sq = sb("sq", [P, ST, H, DH])
            ms, rms = sb("ms", [P, ST, H]), sb("rms", [P, ST, H])
            ON = sb("ON", [P, ST, H, DH])
        else:
            ON = O
            raw_m = sb("raw_m", [P, ST, S], I32)
        psS = [[ps(f"scores{a}{q}") for q in range(ST)] for a in range(2)]
        psT = [ps(f"turned{a}") for a in range(2)]
        psO, psM = ps("summed"), ps("spare")

        opening_banks = (psM, psS[1][0], psS[1][1], psT[0], psM)
        opening_after = (0, 0, 1, 0, 4)

        q_dram, k_dram = (nc.dram_tensor(f"{tag}_{n}_scratch", [2, P, 2, 2 * S], F32).ap() for n in "qk")
        scratch_written = [sem(f"scratch_written{a}") for a in range(2)]
        w_loaded = [sem(f"w_loaded{a}") for a in range(2)]
        w_high, w_split = sem("w_high"), sem("w_split")
        zeroed, passed = sem("zeroed"), sem("passed")
        x_loaded = mem["x_loaded"]
        ctx_loaded, ctx_high, ctx_split = sem("ctx_loaded"), sem("ctx_high"), sem("ctx_split")
        stats_half, stats_ready, eps_added = sem("stats_half"), sem("stats_ready"), sem("eps_added")
        rstd_ready, xn_ready = sem("rstd_ready"), sem("xn_ready")
        bank_filled, bank_emptied = sem("bank_filled"), sem("bank_emptied")
        stack_loaded = [sem(f"stack_loaded{a}") for a in range(2)]
        mask_loaded = [sem(f"mask_loaded{a}") for a in range(MASKS // 2)]
        scores_ready, masked, exp_ready = sem("scores_ready"), sem("masked"), sem("exp_ready")
        rec2_ready, coef_ready, combined = sem("rec2_ready"), sem("coef_ready"), sem("combined")
        turned, head_summed = sem("turned"), sem("head_summed")
        probsT_ready = [sem(f"probsT_ready{a}") for a in range(2)]
        oT_ready, rinv_ready = sem("oT_ready"), sem("rinv_ready")
        squared, ms_ready, ms_scaled, rms_ready, on_ready = (
            sem("squared"), sem("ms_ready"), sem("ms_scaled"), sem("rms_ready"), sem("on_ready"))
        bias_ready, wo_scaled = sem("bias_ready"), sem("wo_scaled")
        high = {n: sem(f"{n}_high") for n in ("xT", "Q", "K", "oT")}
        group_filled, group_emptied = sem("group_filled"), sem("group_emptied")
        split = {"xT": (xT, 1.0), "Q": (q_src, SCALE), "K": (k_src, 1.0), "oT": (OT, 1.0)}

        STACKED = 16 * 12
        HPS, HPH, HPB = layer.heads_per_step, layer.heads_per_half, layer.halves_per_batch
        NV = HPH * DH
        TAIL = BODY if diff else HALF + 1
        LEAVE, WEIGH = (3, 4) if diff else (2, 3)
        PARTS = ((0, 0), (0, 1), (1, 0))
        ctx_v = ctxT.rearrange("(c p) (b t) -> b p c t", p=P, t=S)

        H0, H1 = slice(0, 32 * HALF), slice(32 * HALF, MC)
        LOTS = (((raw_q, Wq, wq, H0), (raw_k, Wk, wk, H0), (raw_v, Wv, wv, slice(0, D))),
                ((raw_q, Wq, wq, H1), (raw_k, Wk, wk, H1))[0:2 * (HPB - 1)] + ((raw_o, Wo, wo, slice(0, D)),))

        def wait(eng, s, value):
            if not isinstance(value, int) or value > 0:
                eng.wait_ge(s, value)

        def hold(eng):
            eng.sem_inc(passed, 1)

        def f32(ap):
            return ap.bitcast(F32)

        def iterations(eng):
            for body, kind in layer.run(eng):
                for i in range(BODY):
                    yield body, kind, i
            for i in range(TAIL):
                yield layer.bodies, DRAIN, i

        def batch_of(body, half):
            return body + half // 2 if diff else 2 * body + half

        def norms(body, kind, i, early, late):
            if diff and i == early and (kind != DRAIN or early == 1):
                return [(2 * body + 1, slice(0, H // 2))]
            if diff and i == late and kind != FIRST:
                return [(2 * body, slice(H // 2, H))]
            return []

        def tenants(body, i, m):
            return BODY * HPS // 2 * body + (HPS * i + m) // 2

        def uses(name, body, rel):
            return batch_of(body, rel) if name in ("xT", "oT") else 2 * body + rel

        block = ctx.enter_context(nc.Block())

        @block.sync
        def _(sp):
            if diff:
                xv = A["x"].rearrange("(n p) d -> p n d", p=P)
                sp.dma_start(X[:, 0:2, :], xv[:, 0:2, :]).then_inc(x_loaded, 16)
            sp.dma_start(raw_c[:], ctx_v[0]).then_inc(ctx_loaded, 16)
            for lot in range(2):
                for raw, _, src, cols in LOTS[lot]:
                    sp.dma_start(raw[:, :, cols], src.rearrange("(c p) n -> p c n", p=P)[:, :, cols])\
                        .then_inc(w_loaded[lot], 16)
            if diff:
                for dst, src in mem["small_loads"]:
                    sp.dma_start(dst, src).then_inc(mem["small_loaded"], 16)
            else:
                sp.dma_start(raw_m[:], mask.rearrange("(t q) k -> q t k", q=P)).then_inc(mask_loaded[0], 16)

            def stack(slot, before):
                wait(sp, stack_loaded[slot], STACKED * before)
                hold(sp)
                for src, scratch in ((q_src, q_dram), (k_src, k_dram)):
                    sp.dma_start(scratch[slot], f32(src[:]).rearrange("p a t s -> p a (t s)"))\
                        .then_inc(scratch_written[slot], 16)
                sp.wait_ge(scratch_written[slot], 32 * (before + 1))
                hold(sp)
                for r, (hq, hk) in enumerate(((0, 0), (0, 1), (1, 0))):
                    for m in range(2):
                        rows = slice(48 * m + 16 * r, 48 * m + 16 * r + 16)
                        for dst, scratch, high in ((q_st[rows, slot, m], q_dram, hq), (k_st[rows, slot], k_dram, hk)):
                            sp.dma_start(f32(dst).rearrange("p (j t) s -> p j (t s)", t=2),
                                         scratch[slot, :, high].rearrange("(j m d) n -> m d j n", m=2, d=DH)[m])\
                                .then_inc(stack_loaded[slot], 16)

            def load_mask(batch, t, i):
                wait(sp, masked, 2 * (t + 2 - MASKS))
                hold(sp)
                sp.dma_start(bias[:, i % MASKS:i % MASKS + 2].rearrange("q h t k -> q (h t) k"),
                             mask[batch, i % H:i % H + 2].rearrange("h (t q) k -> q (h t) k", q=P))\
                    .then_inc(mask_loaded[i // 2 % (MASKS // 2)], 16)

            if diff:
                load_mask(0, 0, 0)
            sp.wait_ge(zeroed, 1)
            sp.wait_ge(bank_emptied, 4)
            stack(0, 0)
            if diff:
                for i in range(2, MASKS - 2, 2):
                    load_mask(0, i, i)
                sp.wait_ge(x_loaded, 16)
                sp.dma_start(X[:, 2:NT, :], xv[:, 2:NT, :]).then_inc(x_loaded, 16)
            else:
                sp.wait_ge(ctx_split, 1)
                sp.dma_start(raw_c[:], ctx_v[1]).then_inc(ctx_loaded, 16)
            sp.wait_ge(zeroed, 2)
            for body, kind, i in iterations(sp):
                t = body * BODY + i
                ahead = i + MASKS - 2
                if diff and i % 2 == 0 and layer.live(i, kind, -(MASKS - 2)) and kind != DRAIN:
                    load_mask(body + ahead // BODY, t + MASKS - 2, ahead)
                for name, half in layer.tasks(i + 3, kind) if i + 3 < BODY else ():
                    if name == "V" and half % HPB == HPB - 1 and layer.exists(half + 1, kind):
                        batch = batch_of(body, half + 1)
                        sp.wait_ge(ctx_split, batch)
                        hold(sp)
                        sp.dma_start(raw_c[:], ctx_v[batch]).then_inc(ctx_loaded, 16)
                for name, half in layer.tasks(i - 1, kind) if i else ():
                    if name == "K":
                        sp.wait_ge(scores_ready, 2 * (body * BODY + HALF * (half - 1)))
                        hold(sp)
                        sp.wait_ge(bank_emptied, layer.number("K", i - 1, kind, body) + 1)
                        hold(sp)
                        stack(half % 2, body + half // 2)

            for dst, src, loaded in next_loads:
                sp.dma_start(dst, src).then_inc(loaded, 16)

        @block.gpsimd
        def _(pool):
            if diff:
                mem["constants"](pool)

            def zero(slot):
                if diff:
                    nc.gpsimd.memset(V[:, slot, :, :, DH:32], 0.0)
                else:
                    nc.gpsimd.memset(V[:, slot, :, :, DH:DH + 1], 1.0)
                    nc.gpsimd.memset(V[:, slot, :, :, DH + 1:32], 0.0)
                nc.gpsimd.memset(f32(q_st[:, slot]), 0.0).then_inc(zeroed, 1)


            def split_ctx(batch):
                pool.wait_ge(ctx_loaded, 16 * (batch + 1))
                hold(pool)
                nc.gpsimd.tensor_copy(cT[:, 0], raw_c[:]).then_inc(ctx_high, 1)
                pool.wait_ge(ctx_high, batch + 1)
                nc.gpsimd.tensor_tensor(cT[:, 1], raw_c[:], f32(cT[:, 0]), ALU.subtract).then_inc(ctx_split, 1)

            def root(batch):
                pool.wait_ge(stats_ready, batch + 1)
                hold(pool)
                nc.gpsimd.tensor_scalar(rstd[:], mv[:, :, 1], EPS, None, ALU.add).then_inc(eps_added, 1)
                pool.wait_ge(eps_added, batch + 1)
                nc.gpsimd.tensor_tensor(rstd[:], rstd[:], mem["minus_half"][:, 0:ST], ALU.pow).then_inc(rstd_ready, 1)

            if diff:
                zero(0)
            root(0)
            split_ctx(0)
            if not diff:
                zero(0)
            if not diff:
                root(1)
            for n, (name, half) in enumerate(layer.opening()):
                if name == "V" and not diff:
                    pool.wait_ge(bank_filled, 4)
                    split_ctx(1)
            zero(1)
            for body, kind, i in iterations(pool):
                for name, half in layer.tasks(i + 3, kind) if i + 3 < BODY else ():
                    if name == "xT":
                        root(batch_of(body, half))
                before = layer.previous(body, kind, i)
                for name, half in layer.tasks(before[2], before[1]) if before else ():
                    past, was, j = before
                    if name == "V" and half % HPB == HPB - 1 and layer.exists(half + 1, was):
                        pool.wait_ge(bank_filled, layer.number("V", j, was, past) + 1)
                        split_ctx(batch_of(past, half + 1))
                for n, heads in norms(body, kind, i, 13, 5):
                    pool.wait_ge(group_emptied, 2 * n)
                    nc.gpsimd.tensor_tensor(sq[:, :, heads, :], O[:, :, heads, :], O[:, :, heads, :], ALU.mult)\
                        .then_inc(squared, 1)
                for n, heads in norms(body, kind, i, 14, 6):
                    pool.wait_ge(ms_ready, n)
                    hold(pool)
                    nc.gpsimd.tensor_scalar(rms[:, :, heads], ms[:, :, heads], 1.0 / DH, EPS, ALU.mult, ALU.add)\
                        .then_inc(ms_scaled, 1)
                    pool.wait_ge(ms_scaled, n)
                for q in range(ST):
                    for n, heads in norms(body, kind, i, 14 + q, 6 + q):
                        nc.gpsimd.tensor_tensor(rms[:, q, heads], rms[:, q, heads], mem["minus_half"][:, 0:H // 2],
                                                ALU.pow).then_inc(rms_ready, 1)

        @block.tensor
        def _(pe):
            def parts(out, left, right, cols_l, cols_r):
                for n, (a, b) in enumerate(PARTS):
                    for c in range(DC):
                        last = nc.tensor.matmul(out, left[:, a, c, cols_l], right[:, b, c, cols_r],
                                                start=(n == 0 and c == 0), stop=(n == 2 and c == DC - 1))
                return last

            def group(batch, g):
                pe.wait_ge(oT_ready, 4 * batch + g + 1)
                for q in range(ST):
                    last = nc.tensor.transpose(psO[:, S + q * P:S + (q + 1) * P], oT[:, q * P:(q + 1) * P], ident[:])
                last.then_inc(group_filled, 1)

            def task(name, rel, batch, n, bank=psM, after=None):
                wait(pe, bank_emptied, n if after is None else after)
                if name == "xT":
                    pe.wait_ge(xn_ready, batch + 1)
                    for q in range(ST):
                        for c in range(DC):
                            last = nc.tensor.transpose(bank[:, c * S + q * P:c * S + (q + 1) * P],
                                                       xn[:, q, c * P:(c + 1) * P], ident[:])
                if name in ("Q", "K"):
                    if name == "K":
                        pe.wait_ge(ctx_split, batch + 1)
                    w, src = (Wq, xT) if name == "Q" else (Wk, cT)
                    for t in range(2):
                        tile = 2 * (rel % HPB) + t
                        last = parts(bank[:, t * S:(t + 1) * S], w, src, slice(tile * P, (tile + 1) * P), slice(0, S))
                if name == "V":
                    pe.wait_ge(ctx_split, batch + 1)
                    for q in range(ST):
                        last = parts(bank[:, q * NV:(q + 1) * NV], cT, Wv, slice(q * P, (q + 1) * P),
                                     slice(rel % HPB * NV, (rel % HPB + 1) * NV))
                if name == "oT":
                    if diff:
                        pe.wait_ge(on_ready, 2 * batch + 2)
                    else:
                        pe.wait_ge(group_emptied, 4 * batch + 4)
                    rows = ON[:].rearrange("p q h d -> p q (h d)")
                    for q in range(ST):
                        for c in range(DC):
                            last = nc.tensor.transpose(bank[:, c * S + q * P:c * S + (q + 1) * P],
                                                       rows[:, q, c * P:(c + 1) * P], ident[:])
                if name == "out":
                    for q in range(ST):
                        last = parts(bank[:, q * D:(q + 1) * D], OT, Wo, slice(q * P, (q + 1) * P), slice(0, D))
                last.then_inc(bank_filled, 1)

            def scores(body, i):
                slot, s = i // HALF, i % HALF
                if s == 0:
                    pe.wait_ge(stack_loaded[slot], STACKED * (body + 1))
                for q in range(ST):
                    wait(pe, masked, 2 * (body * BODY + i - 2) + q + 1)
                    for m in range(2):
                        last = nc.tensor.matmul(psS[i % 2][q][:, m * S:(m + 1) * S],
                                                q_st[:, slot, m, s, q * P:(q + 1) * P], k_st[:, slot, s, :],
                                                start=True, stop=True)
                    last.then_inc(scores_ready, 1)

            def turn(body, i):
                t = body * BODY + i
                for m in range(HPS):
                    u = HPS * t + m
                    place = (HPS * i + m) % 2
                    wait(pe, probsT_ready[place], tenants(body, i, m))
                    if diff:
                        pe.wait_ge(combined, u + 1)
                        rows = comb[:, place]
                    else:
                        pe.wait_ge(exp_ready, 2 * t + 2)
                        rows = Z[:, i % 4, :, m, :]
                    for k in range(ST):
                        for q in range(ST):
                            last = nc.tensor.transpose(psT[place][:, k * S + q * P:k * S + (q + 1) * P],
                                                       rows[:, q, k * P:(k + 1) * P], ident[:])
                    last.then_inc(turned, 1)

            def weigh(body, i):
                for m in range(HPS):
                    u = HPS * (body * BODY + i) + m
                    place, j, v = (HPS * i + m) % 4, (HPS * i + m) % 4, (HPS * i + m) % HPH
                    pe.wait_ge(probsT_ready[place % 2], tenants(body, i, m) + 1)
                    if j == 0:
                        wait(pe, group_emptied, BODY * HPS // 4 * body + HPS * i // 4)
                    for k in range(ST):
                        last = nc.tensor.matmul(psO[32 * j:32 * j + 32, 0:S], V[:, i // HALF % 2, k, v, :],
                                                PT[:, place, k, :], start=(k == 0), stop=(k == ST - 1),
                                                tile_position=(0, 32 * j))
                    last.then_inc(head_summed, 1)

            pe.wait_ge(mem["ident_ready"], 1)
            pe.wait_ge(w_split, len(LOTS[0]))
            for n, (name, half) in enumerate(layer.opening()):
                task(name, half, batch_of(0, half), n, opening_banks[n], opening_after[n])
            scores(0, 0)
            pe.wait_ge(w_split, len(LOTS[0] + LOTS[1]))
            for body, kind, i in iterations(pe):
                t = body * BODY + i
                if kind != DRAIN and layer.live(i, kind, -1):
                    scores(body + (i + 1) // BODY, (i + 1) % BODY)
                if not diff and layer.live(i, kind, 2):
                    turn(body - (i < 2), (i - 2) % BODY)
                for half, g in layer.groups(i, kind):
                    group(batch_of(body, half), g)
                for name, half in layer.tasks(i, kind):
                    task(name, half, batch_of(body, half), layer.number(name, i, kind, body))
                if diff and layer.live(i, kind, 2):
                    turn(body - (i < 2), (i - 2) % BODY)
                if layer.live(i, kind, WEIGH):
                    weigh(body - (i < WEIGH), (i - WEIGH) % BODY)

        @block.scalar
        def _(act):
            def upper_weights(lot):
                act.wait_ge(w_loaded[lot], 16 * len(LOTS[lot]))
                for raw, w, _, cols in LOTS[lot]:
                    if w is Wo and diff:
                        act.wait_ge(wo_scaled, 1)
                    nc.scalar.activation(w[:, 0, :, cols], raw[:, :, cols], ACT.Copy).then_inc(w_high, 1)

            upper_weights(0)

            def task(name, rel, batch, n, body, psum=psM, kind=None):
                if name == "out":
                    return
                act.wait_ge(bank_filled, n + 1)
                bank = psum[:].rearrange("p (a b) -> p a b", a=2)
                if name == "V":
                    act.wait_ge(zeroed, 1 if kind == "opening" else 2)
                    wait(act, head_summed, HPH * (2 * body + rel - 1))
                    for q in range(ST):
                        last = nc.scalar.activation(V[:, rel % 2, q, :, 0:DH],
                                                    psum[:, q * NV:(q + 1) * NV].rearrange("p (h d) -> p h d", d=DH),
                                                    ACT.Copy)
                    last.then_inc(bank_emptied, 1)
                    return
                if name in ("Q", "K"):
                    wait(act, scratch_written[(rel - 1) % 2], 32 * (body + (rel - 1) // 2 + 1))
                dst, scale = split[name]
                nc.scalar.activation(dst[:, 0], bank, ACT.Copy, scale=scale).then_inc(high[name], 1)

            for n, (name, half) in enumerate(layer.opening()):
                task(name, half, batch_of(0, half), n, 0, opening_banks[n], "opening")
            if diff:
                mem["scalar_constants"](act)
            upper_weights(1)
            for body, kind, i in iterations(act):
                t = body * BODY + i

                def exps(q):
                    act.wait_ge(masked, 2 * t + q + 1)
                    for m in range(2):
                        total = {"accum_out": sums[:, i // HALF, i % HALF, q, m:m + 1]} if diff else {}
                        last = nc.scalar.activation(Z[:, i % 4, q, m, :], Z[:, i % 4, q, m, :], ACT.Exp,
                                                    bias=negmax[:, i % 4, q, m:m + 1], scale=-1.0, **total)
                    last.then_inc(exp_ready, 1)

                for half, g in layer.groups(i, kind):
                    act.wait_ge(head_summed, 4 * (4 * batch_of(body, half) + g + 1))
                    nc.scalar.activation(oT[:], psO[:, 0:S], ACT.Copy).then_inc(oT_ready, 1)
                before = layer.previous(body, kind, i)
                for name, half in layer.tasks(before[2], before[1]) if before else ():
                    past, was, j = before
                    task(name, half, batch_of(past, half), layer.number(name, j, was, past), past)
                if kind != DRAIN:
                    exps(0)
                    exps(1)
                if layer.live(i, kind, LEAVE):
                    u = HPS * (t - LEAVE)
                    place = HPS * (i - LEAVE) % 4
                    act.wait_ge(turned, u + 1)
                    wait(act, head_summed, u - 3)
                    nc.scalar.activation(PT[:, place].rearrange("p a b -> p (a b)"), psT[place % 2][:], ACT.Copy)\
                        .then_inc(probsT_ready[place % 2], 1)

        @block.vector
        def _(dve):
            def lower_weights(lot):
                for n, (raw, w, _, cols) in enumerate(LOTS[lot]):
                    dve.wait_ge(w_high, lot * len(LOTS[0]) + n + 1)
                    nc.vector.tensor_tensor(w[:, 1, :, cols], raw[:, :, cols], f32(w[:, 0, :, cols]), ALU.subtract)\
                        .then_inc(w_split, 1)

            def moments(batch):
                if diff:
                    dve.wait_ge(x_loaded, 16 if isinstance(batch, int) and batch == 0 else 32)
                for q in range(ST):
                    last = nc.vector.bn_stats(stats[:, q, :], X[:, bass.ds(2 * batch + q, 1), :])
                last.then_inc(stats_half, 1)
                dve.wait_ge(stats_half, batch + 1)
                hold(dve)
                for q in range(ST):
                    last = nc.vector.bn_aggr(mv[:, q, :], stats[:, q, :])
                last.then_inc(stats_ready, 1)

            def normalise(batch):
                dve.wait_ge(rstd_ready, batch + 1)
                for q in range(ST):
                    last = nc.vector.tensor_scalar(xn[:, q, :], X[:, bass.ds(2 * batch + q, 1), :], mv[:, q, 0:1],
                                                   rstd[:, q:q + 1], ALU.subtract, ALU.mult)
                last.then_inc(xn_ready, 1)

            def group(rel, batch, g):
                turned_sums = psO[:, S:S + ST * P].rearrange("p (q h d) -> p q h d", q=ST, d=32)
                if diff:
                    s = 4 * g % HALF
                    dve.wait_ge(exp_ready, 2 * (4 * (4 * batch + g) + 4))
                    total = sums[:, rel % 2, s:s + 4, :, 0].rearrange("p s q -> p q s")
                else:
                    dve.wait_ge(group_filled, 4 * batch + g + 1)
                    total = turned_sums[:, :, :, DH]
                nc.vector.reciprocal(rinv[:, g % 2], total).then_inc(rinv_ready, 1)
                dve.wait_ge(rinv_ready, 4 * batch + g + 1)
                dve.wait_ge(group_filled, 4 * batch + g + 1)
                nc.vector.tensor_tensor(O[:, :, 4 * g:4 * g + 4, :], turned_sums[:, :, :, 0:DH],
                                        rinv[:, g % 2].unsqueeze(3).to_broadcast([P, ST, 4, DH]), ALU.mult)\
                    .then_inc(group_emptied, 1)

            def task(name, rel, batch, n, body, psum=psM):
                if name in split:
                    dst, scale = split[name]
                    dve.wait_ge(high[name], uses(name, body, rel) + 1)
                    nc.vector.scalar_tensor_tensor(out=dst[:, 1], in0=psum[:].rearrange("p (a b) -> p a b", a=2),
                                                   scalar=scale, in1=f32(dst[:, 0]), op0=ALU.mult, op1=ALU.subtract)\
                        .then_inc(bank_emptied, 1)
                if name == "out":
                    dve.wait_ge(bank_filled, n + 1)
                    rows = X[:, bass.ds(2 * batch, 2), :]
                    nc.vector.scalar_tensor_tensor(out=rows, in0=psM[:].rearrange("p (a b) -> p a b", a=2),
                                                   scalar=gate[:, layer.gate:layer.gate + 1], in1=rows,
                                                   op0=ALU.mult, op1=ALU.add).then_inc(bank_emptied, 1)

            moments(0)
            normalise(0)
            lower_weights(0)
            for n, (name, half) in enumerate(layer.opening()):
                if (name, half) == ("xT", 1):
                    moments(1)
                    normalise(1)
                task(name, half, batch_of(0, half), n, 0, opening_banks[n])
            if diff:
                mem["vector_constants"](dve)
                dve.wait_ge(w_loaded[1], 16 * len(LOTS[1]))
                nc.vector.tensor_scalar(raw_o[:], raw_o[:], mem["rms_col"][:, 0:1], 1.0 - LAMBDA_INIT,
                                        ALU.mult, ALU.mult).then_inc(wo_scaled, 1)
            else:
                dve.wait_ge(mask_loaded[0], 16)
                nc.vector.tensor_scalar(bias[:], raw_m[:], 0.0, MASKED, ALU.is_equal, ALU.mult).then_inc(bias_ready, 1)
            lower_weights(1)
            if not diff:
                dve.wait_ge(bias_ready, 1)
            for body, kind, i in iterations(dve):
                t = body * BODY + i
                late = t - 2
                for q in range(ST):
                    if kind != DRAIN:
                        dve.wait_ge(scores_ready, 2 * t + q + 1)
                    for m in range(2):
                        if kind != DRAIN:
                            if q == 0 and m == 0:
                                if diff:
                                    dve.wait_ge(mask_loaded[i // 2 % (MASKS // 2)], 16 * (BODY // MASKS * body + i // MASKS + 1))
                                else:
                                    wait(dve, turned, HPS * (t - 3))
                            if m == 0 and kind == MIDDLE:
                                hold(dve)
                            last = nc.vector.tensor_tensor_reduce(
                                Z[:, i % 4, q, m, :], psS[i % 2][q][:, m * S:(m + 1) * S],
                                bias[:, i % MASKS, q, :] if diff else bias[:, q, :], -1.0, FLT_MAX, ALU.add, ALU.min,
                                negmax[:, i % 4, q, m:m + 1])
                            if m == 1:
                                last.then_inc(masked, 1)
                        if not diff or not layer.live(i, kind, 2):
                            continue
                        h = (i - 2) % BODY
                        r = sums[:, h // HALF, h % HALF]
                        if (q, m) == (0, 0):
                            dve.wait_ge(exp_ready, 2 * late + 2)
                            nc.vector.reciprocal(rec2[:, h % 2, :], r[:, :, 1]).then_inc(rec2_ready, 1)
                        if (q, m) == (0, 1):
                            dve.wait_ge(rec2_ready, late + 1)
                            nc.vector.scalar_tensor_tensor(out=coef[:, h % 2, :], in0=rec2[:, h % 2, :],
                                                           scalar=mem["minus_lambda"][:, h:h + 1], in1=r[:, :, 0],
                                                           op0=ALU.mult, op1=ALU.mult).then_inc(coef_ready, 1)
                        if q == 1:
                            if m == 0:
                                dve.wait_ge(coef_ready, late + 1)
                                wait(dve, turned, late - 1)
                            last = nc.vector.scalar_tensor_tensor(
                                out=comb[:, h % 2, m, :], in0=Z[:, h % 4, m, 1, :], scalar=coef[:, h % 2, m:m + 1],
                                in1=Z[:, h % 4, m, 0, :], op0=ALU.mult, op1=ALU.add)
                            if m == 1:
                                last.then_inc(combined, 1)
                for name, half in layer.tasks(i + 3, kind) if i + 3 < BODY else ():
                    if name == "xT":
                        moments(batch_of(body, half))
                for name, half in layer.tasks(i + 1, kind) if i + 1 < BODY else ():
                    if name == "xT":
                        normalise(batch_of(body, half))
                for n, heads in norms(body, kind, i, 14, 6):
                    dve.wait_ge(squared, n)
                    nc.vector.tensor_reduce(ms[:, :, heads], sq[:, :, heads, :], AX.X, ALU.add).then_inc(ms_ready, 1)
                for n, heads in norms(body, kind, i, None, 8) + norms(body - 1, kind, i, 1, None):
                    if i == 1 and kind == FIRST:
                        continue
                    dve.wait_ge(rms_ready, 2 * n)
                    nc.vector.tensor_tensor(ON[:, :, heads, :], O[:, :, heads, :],
                                            rms[:, :, heads].unsqueeze(3).to_broadcast([P, ST, H // 2, DH]), ALU.mult)\
                        .then_inc(on_ready, 1)
                def previous_task():
                    before = layer.previous(body, kind, i)
                    for name, half in layer.tasks(before[2], before[1]) if before else ():
                        past, was, j = before
                        task(name, half, batch_of(past, half), layer.number(name, j, was, past), past)

                if not diff:
                    previous_task()
                for half, g in layer.groups(i, kind) if not diff else ():
                    group(half, batch_of(body, half), g)
                if not diff and layer.live(i, kind, LEAVE):
                    u = HPS * (t - LEAVE) + 1
                    dve.wait_ge(turned, u + 1)
                    wait(dve, head_summed, u - 3)
                    nc.vector.tensor_copy(PT[:, (HPS * (i - LEAVE) + 1) % 4].rearrange("p a b -> p (a b)"), psT[1][:]).then_inc(probsT_ready[1], 1)
                for half, g in layer.groups(i, kind) if diff else ():
                    group(half, batch_of(body, half), g)
                if diff:
                    previous_task()


def routed_ffn(nc, A, mem):
    TG = 512
    NG = B * S // TG
    TILES = TG // P
    UC = UH // P
    BODIES = NU // 2
    V_BODY, Q_BODY = 2 * NG, 2 * NG * UC
    with ExitStack() as ctx:
        def sb(name, shape, dt=F32):
            return ctx.enter_context(nc.sbuf_tensor(f"r_{name}", shape, dt))

        def sem(name):
            return ctx.enter_context(nc.semaphore(f"r_{name}"))

        X, ident, gates = mem["x"], mem["ident"], mem["gates"]
        stats, mv = sb("stats", [P, NT, 6]), sb("mv", [P, NT, 2])
        rstd = sb("rstd", [P, NT])
        xn = sb("xn", [P, 2, ST, D])
        xT = sb("xT", [P, 2, DC, B * S], F32R)
        raw_r = sb("raw_r", [P, DC, E])
        Wr = sb("Wr", [P, 2, DC, E], F32R)
        affinity = sb("affinity", [E, B * S])
        scores = sb("scores", [P, NT, E])
        chosen = sb("chosen", [P, NT, E])
        expert_bias = sb("expert_bias", [P, E])
        above, equal = sb("above", [P, NT, E, E]), sb("equal", [P, NT, E, E])
        earlier = sb("earlier", [P, E, E])
        gate = sb("gate", [P, NT, NU])
        raw_up, raw_down = sb("raw_up", [P, 2, DC, 2 * UH]), sb("raw_down", [P, 2, UC, D])
        Wup, Wdown = sb("Wup", [P, 2, 2, DC, 2 * UH], F32R), sb("Wdown", [P, 2, 2, UC, D], F32R)
        silu = sb("silu", [P, 2, TG])
        mixed = sb("mixed", [P, 2, TG])
        hidden = sb("hidden", [P, 2, 2, UC, TG], F32R)
        psH = [[ctx.enter_context(nc.psum_tensor(f"r_up{f}{k}", [P, TG], F32)) for k in range(2)] for f in range(2)]
        psD = [[ctx.enter_context(nc.psum_tensor(f"r_down{a}{k}", [P, 2 * D], F32)) for k in range(2)] for a in range(2)]

        small = sem("small")
        stats_ready, mv_ready, eps_added, rstd_ready = (sem("stats_ready"), sem("mv_ready"), sem("eps_added"),
                                                        sem("rstd_ready"))
        xn_ready, x_turned, x_high, x_split = sem("xn_ready"), sem("x_turned"), sem("x_high"), sem("x_split")
        wr_high, wr_split, routed, affinity_ready = sem("wr_high"), sem("wr_split"), sem("routed"), sem("affinity_ready")
        affinity_turned, chain = sem("affinity_turned"), sem("chain")
        ones_ready, earlier_ready = sem("ones_ready"), sem("earlier_ready")
        w_loaded = [sem(f"w_loaded{a}") for a in range(2)]
        w_part, w_split = sem("w_part"), sem("w_split")
        h1_ready, h2_ready, silu_ready, mixed_ready = sem("h1_ready"), sem("h2_ready"), sem("silu_ready"), sem("mixed_ready")
        high_ready, low_ready, down_ready, x_added = sem("high_ready"), sem("low_ready"), sem("down_ready"), sem("x_added")
        passed = sem("passed")
        PARTS = ((0, 0), (0, 1), (1, 0))

        def f32(ap):
            return ap.bitcast(F32)

        def wait(eng, s, value):
            if not isinstance(value, int) or value > 0:
                eng.wait_ge(s, value)

        def run(eng):
            yield 0, FIRST
            with eng.Fori(1, BODIES - 1) as body:
                yield body, MIDDLE
            yield BODIES - 1, LAST

        def pairs_of_batches(eng):
            for k in range(2):
                yield k, k
            with eng.Fori(1, B // 2) as pair:
                for k in range(2):
                    yield 2 * pair + k, k

        up_v = A["up"].rearrange("u (c p) n -> u p c n", p=P)
        down_v = A["down"].rearrange("u (f p) n -> u p f n", p=P)
        block = ctx.enter_context(nc.Block())

        @block.sync
        def _(sp):
            sp.dma_start(raw_r[:], A["router"].rearrange("(c p) e -> p c e", p=P)).then_inc(small, 16)
            sp.dma_start(expert_bias[:], A["L0_ffn_expert_bias"].partition_broadcast(P)).then_inc(small, 16)

            def load(unit, k):
                sp.dma_start(raw_up[:, k], up_v[unit]).then_inc(w_loaded[k], 16)
                sp.dma_start(raw_down[:, k], down_v[unit]).then_inc(w_loaded[k], 16)

            load(0, 0)
            load(1, 1)
            for body, kind in run(sp):
                for k in range(2):
                    if kind != LAST:
                        sp.wait_ge(w_split, 2 * body + k + 1)
                        sp.sem_inc(passed, 1)
                        load(2 * body + k + 2, k)

        @block.gpsimd
        def _(pool):
            nc.gpsimd.memset(earlier[:], 1.0).then_inc(ones_ready, 1)
            pool.wait_ge(ones_ready, 1)
            nc.gpsimd.affine_select(out=earlier[:], in_=earlier[:], compare_op=ALU.is_gt, fill=0.0, base=0,
                                    pattern=[[1, E], [-1, E]], channel_multiplier=0).then_inc(earlier_ready, 1)

            def split_part(n, k, w_parts):
                if n < 4:
                    raw, w = raw_up[:, k, n // 2], Wup[:, k, :, n // 2]
                else:
                    raw, w = raw_down[:, k], Wdown[:, k]
                if n % 2 == 0:
                    nc.gpsimd.tensor_copy(w[:, 0], raw).then_inc(w_part, 1)
                else:
                    pool.wait_ge(w_part, w_parts)
                    last = nc.gpsimd.tensor_tensor(w[:, 1], raw, f32(w[:, 0]), ALU.subtract)
                    if n == 5:
                        last.then_inc(w_split, 1)

            for lot, tiles in enumerate((slice(0, ST), slice(ST, NT))):
                pool.wait_ge(mv_ready, lot + 1)
                nc.gpsimd.tensor_scalar(rstd[:, tiles], mv[:, tiles, 1], EPS, None, ALU.add).then_inc(eps_added, 1)
                pool.wait_ge(eps_added, lot + 1)
                nc.gpsimd.tensor_tensor(rstd[:, tiles], rstd[:, tiles], mem["minus_half"][:, tiles], ALU.pow)\
                    .then_inc(rstd_ready, 1)
            pool.wait_ge(w_loaded[0], 32)
            for n in range(6):
                split_part(n, 0, n // 2 + 1)
            for body, kind in run(pool):
                for k in range(2):
                    for n in range(NG):
                        for f in range(UC):
                            q = body * Q_BODY + (k * NG + n) * UC + f
                            pool.wait_ge(high_ready, q + 1)
                            nc.gpsimd.tensor_tensor(hidden[:, n % 2, 1, f], mixed[:, f], f32(hidden[:, n % 2, 0, f]),
                                                    ALU.subtract).then_inc(low_ready, 1)
                            part = 2 * n + f - 1
                            if 0 <= part < 6 and not (kind == LAST and k == 1):
                                if part == 0:
                                    pool.wait_ge(w_loaded[1 - k], 32 * (body + k + 1))
                                    wait(pool, down_ready, NG * (2 * body + k))
                                    pool.sem_inc(passed, 1)
                                split_part(part, 1 - k, 3 * (2 * body + k + 1) + part // 2 + 1)

        @block.tensor
        def _(pe):
            for b, k in pairs_of_batches(pe):
                pe.wait_ge(xn_ready, b + 1)
                wait(pe, x_split, b - 1)
                for q in range(ST):
                    for c in range(DC):
                        last = nc.tensor.transpose(psH[k][0][:, c * S + q * P:c * S + (q + 1) * P],
                                                   xn[:, k, q, c * P:(c + 1) * P], ident[:])
                last.then_inc(x_turned, 1)
            pe.wait_ge(x_split, B)
            pe.wait_ge(wr_split, 1)
            for g in range(NG):
                for n, (a, b) in enumerate(PARTS + ((1, 1),)):
                    for c in range(DC):
                        last = nc.tensor.matmul(psD[g // 2][g % 2][0:E, :], Wr[:, a, c, :], xT[:, b, c, g * TG:(g + 1) * TG],
                                                start=(n == 0 and c == 0), stop=(n == 3 and c == DC - 1))
                last.then_inc(routed, 1)
            for t in range(NT):
                pe.wait_ge(affinity_ready, t // TILES + 1)
                last = nc.tensor.transpose(psH[1][1][:, t * E:(t + 1) * E], affinity[:, t * P:(t + 1) * P],
                                           ident[0:E, 0:E])
            last.then_inc(affinity_turned, 1)

            def up(v, k, n, body):
                for f in range(UC):
                    q = UC * v + f
                    wait(pe, mixed_ready, q - 1)
                    for half, ready in ((0, h1_ready), (1, h2_ready)):
                        for m, (a, b) in enumerate(PARTS):
                            for c in range(DC):
                                cols = slice(half * UH + f * P, half * UH + (f + 1) * P)
                                last = nc.tensor.matmul(psH[f][half][:], Wup[:, k, a, c, cols],
                                                        xT[:, b, c, n * TG:(n + 1) * TG],
                                                        start=(m == 0 and c == 0), stop=(m == 2 and c == DC - 1))
                        last.then_inc(ready, 1)

            def down(v, k, n):
                pe.wait_ge(low_ready, UC * v + UC)
                wait(pe, x_added, v - 1)
                for t in range(TILES):
                    for m, (a, b) in enumerate(PARTS):
                        for f in range(UC):
                            last = nc.tensor.matmul(psD[n % 2][t // 2][:, t % 2 * D:(t % 2 + 1) * D],
                                                    hidden[:, n % 2, a, f, t * P:(t + 1) * P], Wdown[:, k, b, f],
                                                    start=(m == 0 and f == 0), stop=(m == 2 and f == UC - 1))
                last.then_inc(down_ready, 1)

            pe.wait_ge(chain, 1)
            for body, kind in run(pe):
                for k in range(2):
                    for n in range(NG):
                        v = body * V_BODY + k * NG + n
                        if n == 0:
                            pe.wait_ge(w_split, 2 * body + k + 1)
                        up(v, k, n, body)
                        if not (kind == FIRST and k == 0 and n == 0):
                            down(v - 1, k if n else 1 - k, (n - 1) % NG)
            down(NU * NG - 1, 1, NG - 1)

        @block.scalar
        def _(act):
            act.wait_ge(small, 32)
            nc.scalar.activation(Wr[:, 0], raw_r[:], ACT.Copy).then_inc(wr_high, 1)
            for b, k in pairs_of_batches(act):
                act.wait_ge(x_turned, b + 1)
                nc.scalar.activation(xT[:, 0, :, bass.ds(S * b, S)], psH[k][0][:].rearrange("p (c s) -> p c s", c=DC),
                                     ACT.Copy).then_inc(x_high, 1)
            for g in range(NG):
                act.wait_ge(routed, g + 1)
                nc.scalar.activation(affinity[:, g * TG:(g + 1) * TG], psD[g // 2][g % 2][0:E, :], ACT.Sigmoid)\
                    .then_inc(affinity_ready, 1)

            def upper_half(v, f, n):
                q = UC * v + f
                act.wait_ge(mixed_ready, q + 1)
                if f == 0:
                    wait(act, down_ready, v - 1)
                nc.scalar.activation(hidden[:, n % 2, 0, f], mixed[:, f], ACT.Copy).then_inc(high_ready, 1)

            for body, kind in run(act):
                for k in range(2):
                    for n in range(NG):
                        v = body * V_BODY + k * NG + n
                        for f in range(UC):
                            q = UC * v + f
                            act.wait_ge(h1_ready, q + 1)
                            wait(act, mixed_ready, q - 1)
                            nc.scalar.activation(silu[:, f], psH[f][0][:], ACT.Silu).then_inc(silu_ready, 1)
                            if not (kind == FIRST and k == n == f == 0):
                                if f:
                                    upper_half(v, 0, n)
                                else:
                                    upper_half(v - 1, 1, (n - 1) % NG)
            upper_half(NU * NG - 1, 1, NG - 1)

        @block.vector
        def _(dve):
            def moments(lot):
                tiles = range(ST) if lot == 0 else range(ST, NT)
                for t in tiles:
                    last = nc.vector.bn_stats(stats[:, t, :], X[:, t, :])
                last.then_inc(stats_ready, 1)
                dve.wait_ge(stats_ready, lot + 1)
                for t in tiles:
                    last = nc.vector.bn_aggr(mv[:, t, :], stats[:, t, :])
                last.then_inc(mv_ready, 1)

            moments(0)
            dve.wait_ge(wr_high, 1)
            nc.vector.tensor_tensor(Wr[:, 1], raw_r[:], f32(Wr[:, 0]), ALU.subtract).then_inc(wr_split, 1)
            dve.wait_ge(rstd_ready, 1)

            def lower_half(b, k):
                dve.wait_ge(x_high, b + 1)
                nc.vector.tensor_tensor(xT[:, 1, :, bass.ds(S * b, S)], psH[k][0][:].rearrange("p (c s) -> p c s", c=DC),
                                        f32(xT[:, 0, :, bass.ds(S * b, S)]), ALU.subtract).then_inc(x_split, 1)

            for b, k in pairs_of_batches(dve):
                wait(dve, x_turned, b - 1)
                for q in range(ST):
                    t = 2 * b + q
                    last = nc.vector.tensor_scalar(xn[:, k, q, :], X[:, bass.ds(t, 1), :], mv[:, bass.ds(t, 1), 0],
                                                   rstd[:, bass.ds(t, 1)], ALU.subtract, ALU.mult)
                last.then_inc(xn_ready, 1)
                if isinstance(b, int) and b == 0:
                    moments(1)
                    dve.wait_ge(rstd_ready, 2)
                else:
                    lower_half(b - 1, 1 - k)
            lower_half(B - 1, 1)
            step = [0]

            def then(ins):
                step[0] += 1
                ins.then_inc(chain, 1)
                dve.wait_ge(chain, step[0])

            dve.wait_ge(affinity_turned, 1)
            then(nc.vector.tensor_copy(scores[:].rearrange("p t e -> p (t e)"), psH[1][1][:, 0:NT * E]))
            dve.wait_ge(small, 32)
            then(nc.vector.tensor_tensor(chosen[:], scores[:], expert_bias[:].unsqueeze(1).to_broadcast([P, NT, E]),
                                         ALU.add))
            other = chosen[:].unsqueeze(2).to_broadcast([P, NT, E, E])
            own = chosen[:].unsqueeze(3).to_broadcast([P, NT, E, E])
            then(nc.vector.tensor_tensor(above[:], other, own, ALU.is_gt))
            then(nc.vector.tensor_tensor(equal[:], other, own, ALU.is_equal))
            dve.wait_ge(earlier_ready, 1)
            then(nc.vector.tensor_tensor(equal[:], equal[:], earlier[:].unsqueeze(1).to_broadcast([P, NT, E, E]),
                                         ALU.mult))
            then(nc.vector.tensor_tensor(above[:], above[:], equal[:], ALU.add))
            then(nc.vector.tensor_reduce(chosen[:], above[:], AX.X, ALU.add))
            then(nc.vector.tensor_scalar(chosen[:], chosen[:], 1.5, None, ALU.is_lt))
            then(nc.vector.scalar_tensor_tensor(out=gate[:, :, NU - E:NU], in0=chosen[:], scalar=gates[:, 2:3],
                                                in1=scores[:], op0=ALU.mult, op1=ALU.mult))
            then(nc.vector.memset(gate[:, :, 0:NU - E], 1.0))
            then(nc.vector.tensor_scalar(gate[:, :, 0:NU - E], gate[:, :, 0:NU - E], gates[:, 2:3], None, ALU.mult))

            def add(v, unit_k, n, body):
                dve.wait_ge(down_ready, v + 1)
                for t in range(TILES):
                    rows = X[:, n * TILES + t, :]
                    last = nc.vector.scalar_tensor_tensor(
                        out=rows, in0=psD[n % 2][t // 2][:, t % 2 * D:(t % 2 + 1) * D],
                        scalar=gate[:, n * TILES + t, bass.ds(2 * body + unit_k, 1)], in1=rows, op0=ALU.mult, op1=ALU.add)
                last.then_inc(x_added, 1)

            for body, kind in run(dve):
                for k in range(2):
                    for n in range(NG):
                        v = body * V_BODY + k * NG + n
                        for f in range(UC):
                            q = UC * v + f
                            dve.wait_ge(silu_ready, q + 1)
                            dve.wait_ge(h2_ready, q + 1)
                            wait(dve, low_ready, q - 1)
                            nc.vector.tensor_tensor(mixed[:, f], psH[f][1][:], silu[:, f], ALU.mult)\
                                .then_inc(mixed_ready, 1)
                        if not (kind == FIRST and k == 0 and n == 0):
                            add(v - 1, k if n else k - 1, (n - 1) % NG, body)
            add(NU * NG - 1, 1, NG - 1, BODIES - 1)


def expert_ffn(nc, A, mem, W1, W2, w_loaded):
    FC = FF // P
    with ExitStack() as ctx:
        def sb(name, shape, dt=F32):
            return ctx.enter_context(nc.sbuf_tensor(f"e_{name}", shape, dt))

        def sem(name):
            return ctx.enter_context(nc.semaphore(f"e_{name}"))

        X, ident, gates = mem["x"], mem["ident"], mem["gates"]
        stats, mv = sb("stats", [P, NT, 6]), sb("mv", [P, NT, 2])
        rstd = sb("rstd", [P, NT])
        xn = sb("xn", [P, 2, ST, D])
        xT = sb("xT", [P, 2, DC, S])
        b1_rows, b1 = sb("b1_rows", [E * FC, P]), sb("b1", [P, E * FC])
        b2 = sb("b2", [1, E, D])
        ones = sb("ones", [1, P])
        hidden = sb("hidden", [P, 2, FC, S])
        psX = [ctx.enter_context(nc.psum_tensor(f"e_x{a}", [P, DC * S], F32)) for a in range(2)]
        psH = [ctx.enter_context(nc.psum_tensor(f"e_h{a}", [P, 512], F32)) for a in range(4)]
        psY = [ctx.enter_context(nc.psum_tensor(f"e_y{a}", [P, ST * D], F32)) for a in range(2)]
        small, ones_ready, b1_turned, b1_ready = sem("small"), sem("ones_ready"), sem("b1_turned"), sem("b1_ready")
        stats_ready, mv_ready, eps_added, rstd_ready = (sem("stats_ready"), sem("mv_ready"), sem("eps_added"),
                                                        sem("rstd_ready"))
        xn_ready, x_turned, xT_ready = sem("xn_ready"), sem("x_turned"), sem("xT_ready")
        h_ready, gelu_ready, y_ready, x_added, saved = (sem("h_ready"), sem("gelu_ready"), sem("y_ready"),
                                                        sem("x_added"), sem("saved"))
        passed = sem("passed")

        def wait(eng, s, value):
            if not isinstance(value, int) or value > 0:
                eng.wait_ge(s, value)

        def pairs(eng):
            for k in range(2):
                yield k, k
            with eng.Fori(1, B // 2) as pair:
                for k in range(2):
                    yield 2 * pair + k, k

        w1_v = A["L1_ffn_w1"].rearrange("e (c p) n -> e p c n", p=P)
        w2_v = A["L1_ffn_w2"].rearrange("e (f p) n -> e p f n", p=P)
        out_v = A["out"].rearrange("(b q p) d -> b p q d", p=P, q=ST)
        block = ctx.enter_context(nc.Block())

        def save(sp, b):
            sp.wait_ge(x_added, b + 1)
            sp.sem_inc(passed, 1)
            sp.dma_start(out_v[b], X[:, bass.ds(2 * b, 2), :]).then_inc(saved, 16)

        @block.sync
        def _(sp):
            sp.dma_start(b1_rows[:], A["L1_ffn_b1"].rearrange("e (f p) -> (e f) p", p=P)).then_inc(small, 16)
            sp.dma_start(b2[:], A["L1_ffn_b2"].rearrange("(a e) d -> a e d", a=1)).then_inc(small, 16)
            for b, k in pairs(sp):
                if not isinstance(b, int):
                    sp.wait_ge(y_ready, b - 1)
                    sp.sem_inc(passed, 1)
                    sp.dma_start(W1[:, k], w1_v[b]).then_inc(w_loaded[k], 16)
                    sp.dma_start(W2[:, k], w2_v[b]).then_inc(w_loaded[k], 16)
                if isinstance(b, int) and b < 1:
                    continue
                save(sp, b - 1)
            save(sp, B - 1)
            sp.wait_ge(saved, 16 * B)

        @block.gpsimd
        def _(pool):
            nc.gpsimd.memset(ones[:], 1.0).then_inc(ones_ready, 1)
            for lot, tiles in enumerate((slice(0, ST), slice(ST, NT))):
                pool.wait_ge(mv_ready, lot + 1)
                nc.gpsimd.tensor_scalar(rstd[:, tiles], mv[:, tiles, 1], EPS, None, ALU.add).then_inc(eps_added, 1)
                pool.wait_ge(eps_added, lot + 1)
                nc.gpsimd.tensor_tensor(rstd[:, tiles], rstd[:, tiles], mem["minus_half"][:, tiles], ALU.pow)\
                    .then_inc(rstd_ready, 1)

        @block.tensor
        def _(pe):
            pe.wait_ge(small, 32)
            pe.wait_ge(ones_ready, 1)
            nc.tensor.transpose(psY[1][:, 0:E * FC], b1_rows[:], ident[0:E * FC, 0:E * FC]).then_inc(b1_turned, 1)

            def turn(b, k):
                pe.wait_ge(xn_ready, b + 1)
                for q in range(ST):
                    for c in range(DC):
                        last = nc.tensor.transpose(psX[k][:, c * S + q * P:c * S + (q + 1) * P],
                                                   xn[:, k, q, c * P:(c + 1) * P], ident[:])
                last.then_inc(x_turned, 1)

            for b, k in pairs(pe):
                turn(b, k)
                pe.wait_ge(xT_ready, b + 1)
                pe.wait_ge(w_loaded[k], 32 * (b // 2 + 1) if isinstance(b, int) else 16 * (b - k + 2))
                for f in range(FC):
                    wait(pe, gelu_ready, FC * b + f - 7 + f % 2)
                    for c in range(DC):
                        last = nc.tensor.matmul(psH[f // 2][:, f % 2 * S:(f % 2 + 1) * S],
                                                W1[:, k, c, f * P:(f + 1) * P], xT[:, k, c, :],
                                                start=(c == 0), stop=(c == DC - 1))
                    if f % 2:
                        last.then_inc(h_ready, 1)
                wait(pe, x_added, b - 1)
                if isinstance(b, int) and b == 1:
                    pe.wait_ge(b1_ready, 1)
                for q in range(ST):
                    out = psY[k][:, q * D:(q + 1) * D]
                    for f in range(FC):
                        pe.wait_ge(gelu_ready, FC * b + f + 1)
                        nc.tensor.matmul(out, hidden[:, k, f, q * P:(q + 1) * P], W2[:, k, f, :],
                                         start=(f == 0), stop=False)
                    last = nc.tensor.matmul(out, ones[:], b2[:, bass.ds(b, 1), :], start=False, stop=True)
                last.then_inc(y_ready, 1)

        @block.scalar
        def _(act):
            act.wait_ge(b1_turned, 1)
            nc.scalar.activation(b1[:], psY[1][:, 0:E * FC], ACT.Copy).then_inc(b1_ready, 1)
            for b, k in pairs(act):
                act.wait_ge(x_turned, b + 1)
                wait(act, y_ready, b - 1)
                nc.scalar.activation(xT[:, k].rearrange("p c s -> p (c s)"), psX[k][:], ACT.Copy).then_inc(xT_ready, 1)
                act.wait_ge(b1_ready, 1)
                for f in range(FC):
                    act.wait_ge(h_ready, FC // 2 * b + f // 2 + 1)
                    nc.scalar.activation(hidden[:, k, f, :], psH[f // 2][:, f % 2 * S:(f % 2 + 1) * S],
                                         ACT.Gelu_apprx_tanh, bias=b1[:, bass.ds(FC * b + f, 1)])\
                        .then_inc(gelu_ready, 1)

        @block.vector
        def _(dve):
            def moments(lot):
                tiles = range(ST) if lot == 0 else range(ST, NT)
                for t in tiles:
                    last = nc.vector.bn_stats(stats[:, t, :], X[:, t, :])
                last.then_inc(stats_ready, 1)
                dve.wait_ge(stats_ready, lot + 1)
                for t in tiles:
                    last = nc.vector.bn_aggr(mv[:, t, :], stats[:, t, :])
                last.then_inc(mv_ready, 1)

            moments(0)
            dve.wait_ge(rstd_ready, 1)

            def normalise(b, k):
                wait(dve, x_turned, b - 1)
                for q in range(ST):
                    t = 2 * b + q
                    last = nc.vector.tensor_scalar(xn[:, k, q, :], X[:, bass.ds(t, 1), :], mv[:, bass.ds(t, 1), 0],
                                                   rstd[:, bass.ds(t, 1)], ALU.subtract, ALU.mult)
                last.then_inc(xn_ready, 1)

            def add(b, k):
                dve.wait_ge(y_ready, b + 1)
                rows = X[:, bass.ds(2 * b, 2), :]
                nc.vector.scalar_tensor_tensor(out=rows, in0=psY[k][:].rearrange("p (q d) -> p q d", q=ST),
                                               scalar=gates[:, 3:4], in1=rows, op0=ALU.mult, op1=ALU.add)\
                    .then_inc(x_added, 1)

            for b, k in pairs(dve):
                normalise(b, k)
                if isinstance(b, int) and b == 0:
                    moments(1)
                    dve.wait_ge(rstd_ready, 2)
                else:
                    add(b - 1, 1 - k)
            add(B - 1, 1)


def prepare(nc, A, mem):
    small_loaded, ramp, ident_ready, const_ready, lam_ready, gate_ready = (
        mem["small_loaded"], mem["ramp"], mem["ident_ready"], mem["const_ready"], mem["lam_ready"], mem["gate_ready"])

    def constants(pool):
        nc.gpsimd.memset(mem["ident"][:], 0.0).then_inc(ramp, 1)
        nc.gpsimd.memset(mem["minus_half"][:], -0.5).then_inc(ramp, 1)
        pool.wait_ge(ramp, 2)
        nc.gpsimd.affine_select(out=mem["ident"][:], in_=mem["ident"][:], compare_op=ALU.not_equal, fill=1.0, base=0,
                                pattern=[[-1, P]], channel_multiplier=1).then_inc(ident_ready, 1)

    def vector_constants(dve):
        lam, dots = mem["lam"], mem["dots"]
        dve.wait_ge(small_loaded, 16 * len(mem["small_loads"]))
        for n in range(2):
            nc.vector.tensor_tensor(lam[:, 2 * n, :], lam[:, 2 * n, :], lam[:, 2 * n + 1, :], ALU.mult)\
                .then_inc(lam_ready, 1)
        dve.wait_ge(lam_ready, 2)
        for n in range(2):
            nc.vector.tensor_reduce(dots[:, n, :], lam[:, 2 * n, :].rearrange("p (h d) -> p h d", d=DH), AX.X, ALU.add)\
                .then_inc(lam_ready, 1)
        dve.wait_ge(const_ready, 1)
        nc.vector.tensor_tensor(mem["minus_lambda"][:], dots[:, 1, :], dots[:, 0, :], ALU.subtract).then_inc(lam_ready, 1)
        dve.wait_ge(lam_ready, 5)
        nc.vector.tensor_scalar(mem["minus_lambda"][:], mem["minus_lambda"][:], LAMBDA_INIT, None, ALU.subtract)\
            .then_inc(lam_ready, 1)
        dve.wait_ge(lam_ready, 6)
        dve.wait_ge(gate_ready, 1)

    def scalar_constants(act):
        act.wait_ge(lam_ready, 4)
        nc.scalar.activation(mem["dots"][:], mem["dots"][:], ACT.Exp).then_inc(const_ready, 1)
        nc.scalar.activation(mem["gates"][:], mem["gates"][:], ACT.Tanh).then_inc(gate_ready, 1)

    mem["constants"], mem["vector_constants"], mem["scalar_constants"] = constants, vector_constants, scalar_constants


def build(nc, A, stop=None):
    with ExitStack() as ctx:
        def sb(name, shape, dt=F32):
            return ctx.enter_context(nc.sbuf_tensor(name, shape, dt))

        mem = {"x": sb("x", [P, NT, D]), "ident": sb("ident", [P, P]), "minus_half": sb("minus_half", [P, 32]),
               "gates": sb("gates", [P, 4]), "lam": sb("lam", [P, 4, H * DH]), "dots": sb("dots", [P, 2, H]),
               "minus_lambda": sb("minus_lambda", [P, H]), "rms_col": sb("rms_col", [P, 1])}
        for name in ("small_loaded", "ramp", "ident_ready", "const_ready", "lam_ready", "gate_ready", "x_loaded",
                     "saved"):
            mem[name] = ctx.enter_context(nc.semaphore(name))
        row = lambda a: a.partition_broadcast(P)
        mem["small_loads"] = [(mem["lam"][:, n, :], row(A[f"L0_xattn_lambda_{w}"].rearrange("h d -> (h d)")))
                              for n, w in enumerate(("q1", "k1", "q2", "k2"))]
        mem["small_loads"] += [(mem["gates"][:, 0:2], row(A["g_xattn"])), (mem["gates"][:, 2:4], row(A["g_ffn"]))]
        mem["small_loads"] += [(mem["rms_col"][DH * n:DH * (n + 1), :], A["L0_xattn_rms_scale"].rearrange("(d a) -> d a", a=1))
                               for n in range(P // DH)]
        prepare(nc, A, mem)
        first, second = Layer(True), Layer(False)
        first.gate, second.gate = 0, 1
        attention(nc, A, first, mem, A["ctxT"], A["mask_full"], A["L0_wq"], A["L0_wk"], A["L0_wv"], A["L0_wo"])
        if stop != "d":
            routed_ffn(nc, A, mem)
        if stop not in ("d", "r"):
            w1 = sb("expert_w1", [P, 2, DC, FF])
            w2 = sb("expert_w2", [P, 2, FF // P, D])
            w_loaded = [ctx.enter_context(nc.semaphore(f"expert_w_loaded{k}")) for k in range(2)]
            loads = [(w[:, k], A[f"L1_ffn_{n}"][k].rearrange("(c p) n -> p c n", p=P), w_loaded[k])
                     for k in range(2) for n, w in (("w1", w1), ("w2", w2))]
            attention(nc, A, second, mem, A["ctxT"], A["mask_keys"], A["L1_wq"], A["L1_wk"], A["L1_wv"], A["L1_wo"],
                      loads)
        if stop is None:
            expert_ffn(nc, A, mem, w1, w2, w_loaded)
            return
        with nc.Block() as block:
            @block.sync
            def _(sp):
                sp.dma_start(A["out"].rearrange("(n p) d -> p n d", p=P), mem["x"][:]).then_inc(mem["saved"], 16)
                sp.wait_ge(mem["saved"], 16)


def tiled(w):
    return w.reshape(D, -1, 4, 2, 32).transpose(0, 1, 3, 2, 4).reshape(D, -1)


def layout(x, ctx_1024, mask_Bx16xSxS2_ff0, mask_1x1xSxS2_ik0, g_xattn, g_ffn, **w):
    import numpy as np

    turn = lambda a: np.swapaxes(a, -1, -2)
    up = [np.concatenate([turn(w["L0_ffn_shared_w1"])[:, u * UH:(u + 1) * UH],
                          turn(w["L0_ffn_shared_w2"])[:, u * UH:(u + 1) * UH]], 1) for u in range(FF // UH)]
    down = [turn(w["L0_ffn_shared_w3"])[u * UH:(u + 1) * UH] for u in range(FF // UH)]
    arrays = {
        "x": x.reshape(B * S, D), "ctxT": turn(ctx_1024.reshape(B * S, D)), "mask_full": mask_Bx16xSxS2_ff0,
        "mask_keys": mask_1x1xSxS2_ik0[0, 0], "g_xattn": g_xattn, "g_ffn": g_ffn,
        "L0_wq": tiled(w["L0_xattn_W_q"]), "L0_wk": tiled(w["L0_xattn_W_k"]),
        "L0_wv": w["L0_xattn_W_v"], "L0_wo": w["L0_xattn_W_o"],
        "L1_wq": tiled(turn(w["L1_xattn_W_q"])), "L1_wk": tiled(turn(w["L1_xattn_W_k"])),
        "L1_wv": turn(w["L1_xattn_W_v"]), "L1_wo": turn(w["L1_xattn_W_o"]),
        "up": np.concatenate([np.stack(up), turn(w["L0_ffn_w12"])]),
        "down": np.concatenate([np.stack(down), turn(w["L0_ffn_w3"])]),
        "router": turn(w["L0_ffn_router_w"]),
    }
    for name in ("L0_xattn_lambda_q1", "L0_xattn_lambda_k1", "L0_xattn_lambda_q2", "L0_xattn_lambda_k2",
                 "L0_xattn_rms_scale", "L0_ffn_expert_bias", "L1_ffn_w1", "L1_ffn_b1", "L1_ffn_w2", "L1_ffn_b2"):
        arrays[name] = w[name]
    return {name: np.ascontiguousarray(a) for name, a in arrays.items()}


def kernel(**inputs):
    import numpy as np
    import concourse.bacc as bacc
    from concourse.bass_utils import run_bass_kernel_spmd

    nc = bacc.Bacc("TRN2", target_bir_lowering=False, num_devices=1)
    arrays = {f"in_{n}": a for n, a in layout(**{n: np.asarray(a) for n, a in inputs.items()}).items()}
    A = {n[3:]: nc.dram_tensor(n, a.shape, mybir.dt.from_np(a.dtype), kind="ExternalInput").ap()
         for n, a in arrays.items()}
    A["out"] = nc.dram_tensor("out", (B * S, D), F32, kind="ExternalOutput").ap()
    build(nc, A)
    r = run_bass_kernel_spmd(nc, [arrays], core_ids=[0])
    return r.results[0]["out"].reshape(B, S, D)
```
